# Optimizing a Trainium2 kernel written in Bass

```python
import numpy as np
import jax
import jax.numpy as jnp

def _softmax(x, axis=-1):
    return jax.nn.softmax(x, axis=axis)

def _gelu(x):
    return jax.nn.gelu(x, approximate=True)

def _silu(x):
    return jax.nn.silu(x)

def _sigmoid(x):
    return jax.nn.sigmoid(x)

def _layernorm(x, axis=-1, eps=1e-05):
    m = jnp.mean(x, axis=axis, keepdims=True)
    v = jnp.var(x, axis=axis, keepdims=True)
    return (x - m) / jnp.sqrt(v + eps)

def _scatter_add(tgt, idx, src, axis=0):
    return tgt.at[idx].add(src)

def _segment_sum(src, seg, n):
    return jax.ops.segment_sum(src, seg, n)
kernel_name = 'mk_adj_ffn_d1_adj_r2_0fd562'

def setup_inputs(seed: int=0):
    np.random.seed(seed)
    _w = jnp.asarray

    def _rec_inputs():
        import jax
        import jax.numpy as jnp
        _gk = jax.random.key(seed)
        x = -0.0002928 + 1 * jax.random.normal(jax.random.fold_in(_gk, 1), (16, 512, 256), jnp.float32)
        _a = jax.random.bernoulli(jax.random.fold_in(_gk, 2), 0.015625, (16, 512, 512))
        adj = _a
        return (x, adj)
    x, adj = _rec_inputs()

    def _L0_gnn_setup():
        import jax, jax.numpy as jnp
        import numpy as np
        QUERY_DIM = 256
        HEADS = 4
        DIM_HEAD = 64
        INNER = HEADS * DIM_HEAD
        B, N = (4, 1024)
        key = jax.random.key(seed)
        ks = jax.random.split(key, 6)
        s = 1.0 / np.sqrt(QUERY_DIM)
        x = jax.random.normal(ks[0], (B, N, QUERY_DIM), dtype=jnp.float32)
        adjacency_mask = jax.random.randint(ks[1], (B, N, N), 0, 2) > 0
        Wq = jax.random.normal(ks[2], (QUERY_DIM, INNER), dtype=jnp.float32) * s
        Wk = jax.random.normal(ks[3], (QUERY_DIM, INNER), dtype=jnp.float32) * s
        Wv = jax.random.normal(ks[4], (QUERY_DIM, INNER), dtype=jnp.float32) * s
        Wo = jax.random.normal(ks[5], (INNER, QUERY_DIM), dtype=jnp.float32) * (1.0 / np.sqrt(INNER))
        bo = jnp.zeros((QUERY_DIM,), dtype=jnp.float32)
        return {'x': x, 'adjacency_mask': adjacency_mask, 'Wq': Wq, 'Wk': Wk, 'Wv': Wv, 'Wo': Wo, 'bo': bo}
    _L0_gnn_all = _L0_gnn_setup()
    _L0_gnn_in = {k: v for k, v in _L0_gnn_all.items() if k in ('Wq', 'Wk', 'Wv', 'Wo', 'bo')}
    del _L0_gnn_all

    def _L0_ffn_setup():
        import jax, jax.numpy as jnp
        import numpy as np
        MICRO_BATCHES = 2
        TOP_K = 2
        D = 256
        E = 8
        B, S = (8, 4096)
        key = jax.random.key(seed)
        ks = jax.random.split(key, 12)
        s = 0.02
        return {'x': jax.random.normal(ks[0], (B, S, D), dtype=jnp.float32), 'ln_g': jnp.ones((D,), jnp.float32), 'ln_b': jnp.zeros((D,), jnp.float32), 'attn_w': jax.random.normal(ks[1], (D, D), jnp.float32) * s, 'attn_b': jnp.zeros((D,), jnp.float32), 'gate_w': jax.random.normal(ks[2], (E, D), jnp.float32) * s, 'fc1_w': jax.random.normal(ks[3], (E, 4 * D, D), jnp.float32) * s, 'fc1_b': jnp.zeros((E, 4 * D), jnp.float32), 'fc2_w': jax.random.normal(ks[4], (E, D, 4 * D), jnp.float32) * s, 'fc2_b': jnp.zeros((E, D), jnp.float32), 'next_w': jax.random.normal(ks[5], (D, D), jnp.float32) * s, 'next_b': jnp.zeros((D,), jnp.float32)}
    _L0_ffn_all = _L0_ffn_setup()
    _L0_ffn_in = {k: v for k, v in _L0_ffn_all.items() if k in ('ln_g', 'ln_b', 'attn_w', 'attn_b', 'gate_w', 'fc1_w', 'fc1_b', 'fc2_w', 'fc2_b', 'next_w', 'next_b')}
    del _L0_ffn_all
    return {'x': x, 'adj': adj, 'L0_gnn_Wq': _L0_gnn_in['Wq'], 'L0_gnn_Wk': _L0_gnn_in['Wk'], 'L0_gnn_Wv': _L0_gnn_in['Wv'], 'L0_gnn_Wo': _L0_gnn_in['Wo'], 'L0_gnn_bo': _L0_gnn_in['bo'], 'L0_ffn_ln_g': _L0_ffn_in['ln_g'], 'L0_ffn_ln_b': _L0_ffn_in['ln_b'], 'L0_ffn_attn_w': _L0_ffn_in['attn_w'], 'L0_ffn_attn_b': _L0_ffn_in['attn_b'], 'L0_ffn_gate_w': _L0_ffn_in['gate_w'], 'L0_ffn_fc1_w': _L0_ffn_in['fc1_w'], 'L0_ffn_fc1_b': _L0_ffn_in['fc1_b'], 'L0_ffn_fc2_w': _L0_ffn_in['fc2_w'], 'L0_ffn_fc2_b': _L0_ffn_in['fc2_b'], 'L0_ffn_next_w': _L0_ffn_in['next_w'], 'L0_ffn_next_b': _L0_ffn_in['next_b']}

def reference(x, adj, L0_gnn_Wq, L0_gnn_Wk, L0_gnn_Wv, L0_gnn_Wo, L0_gnn_bo, L0_ffn_ln_g, L0_ffn_ln_b, L0_ffn_attn_w, L0_ffn_attn_b, L0_ffn_gate_w, L0_ffn_fc1_w, L0_ffn_fc1_b, L0_ffn_fc2_w, L0_ffn_fc2_b, L0_ffn_next_w, L0_ffn_next_b):
    import jax
    import jax.numpy as jnp

    def _L0_gnn_ref(x, adjacency_mask, Wq, Wk, Wv, Wo, bo):
        import jax, jax.numpy as jnp
        import numpy as np
        QUERY_DIM = 256
        HEADS = 4
        DIM_HEAD = 64
        INNER = HEADS * DIM_HEAD
        B, N = (4, 1024)
        scale = DIM_HEAD ** (-0.5)

        def split_heads(t):
            b, n, _ = t.shape
            return t.reshape(b, n, HEADS, DIM_HEAD).transpose(0, 2, 1, 3)
        q = split_heads(x @ Wq)
        k = split_heads(x @ Wk)
        v = split_heads(x @ Wv)
        sim = jnp.einsum('bhid,bhjd->bhij', q, k) * scale
        neg = -jnp.finfo(sim.dtype).max
        sim = jnp.where(adjacency_mask[:, None, :, :], sim, neg)
        attn = jax.nn.softmax(sim, axis=-1)
        out = jnp.einsum('bhij,bhjd->bhid', attn, v)
        out = out.transpose(0, 2, 1, 3).reshape(x.shape[0], x.shape[1], INNER)
        return out @ Wo + bo

    def _L0_ffn_ref(x, ln_g, ln_b, attn_w, attn_b, gate_w, fc1_w, fc1_b, fc2_w, fc2_b, next_w, next_b):
        import jax, jax.numpy as jnp
        import numpy as np
        MICRO_BATCHES = 2
        TOP_K = 2
        D = 256
        E = 8
        B, S = (8, 4096)
        b, s, d = x.shape
        xf = x.reshape(b * s, d)
        mu = jnp.mean(xf, axis=-1, keepdims=True)
        var = jnp.var(xf, axis=-1, keepdims=True)
        normed = (xf - mu) / jnp.sqrt(var + 1e-05) * ln_g + ln_b
        x_attn = normed @ attn_w.T + attn_b + xf
        logits = x_attn @ gate_w.T
        _scores, _indices = jax.lax.top_k(logits, TOP_K)
        e = fc1_w.shape[0]
        t = b * s // (MICRO_BATCHES * e)
        tok = x_attn.reshape(MICRO_BATCHES, e, t, d)
        h = jnp.einsum('meti,ehi->meth', tok, fc1_w) + fc1_b[None, :, None, :]
        h = jax.nn.gelu(h, approximate=False)
        y = jnp.einsum('meth,edh->metd', h, fc2_w) + fc2_b[None, :, None, :]
        yf = y.reshape(b * s, d)
        out = jax.nn.gelu(yf @ next_w.T + next_b, approximate=False)
        return out.reshape(b, s, d)
    x = x + _L0_gnn_ref(_layernorm(x, axis=-1), adj, L0_gnn_Wq, L0_gnn_Wk, L0_gnn_Wv, L0_gnn_Wo, L0_gnn_bo)
    x = x + _L0_ffn_ref(_layernorm(x, axis=-1), L0_ffn_ln_g, L0_ffn_ln_b, L0_ffn_attn_w, L0_ffn_attn_b, L0_ffn_gate_w, L0_ffn_fc1_w, L0_ffn_fc1_b, L0_ffn_fc2_w, L0_ffn_fc2_b, L0_ffn_next_w, L0_ffn_next_b)
    return x

_drawn_inputs = setup_inputs


def setup_inputs(seed=0):
    import zlib

    import numpy as np

    out = dict(_drawn_inputs(seed))
    spreads = {'L0_gnn_bo': (0.0, 0.1),
     'L0_ffn_ln_g': (1.0, 0.6),
     'L0_ffn_ln_b': (0.0, 0.8),
     'L0_ffn_attn_b': (0.0, 0.8),
     'L0_ffn_fc1_b': (0.0, 0.8),
     'L0_ffn_fc2_b': (0.0, 0.563),
     'L0_ffn_next_b': (0.0, 0.1)}
    factors = {'L0_ffn_attn_w': 8.0, 'L0_ffn_fc1_w': 3.368, 'L0_ffn_fc2_w': 3.174}
    for name, (base, spread) in spreads.items():
        noise = np.random.default_rng([zlib.crc32(name.encode()), seed]).standard_normal(out[name].shape)
        drawn = base * np.exp(spread * noise) if base else spread * noise
        out[name] = jnp.asarray(drawn.astype(out[name].dtype))
    for name, factor in factors.items():
        out[name] = (out[name] * factor).astype(out[name].dtype)
    return out
```

```python
from contextlib import ExitStack

import concourse.bass as bass
from concourse import mybir
from concourse.alu_op_type import AluOpType as ALU

F32 = mybir.dt.float32
F32R = mybir.dt.float32r
BF16 = mybir.dt.bfloat16
U8 = mybir.dt.uint8
U32 = mybir.dt.uint32
ACT = mybir.ActivationFunctionType

P = 128
EPS = 1e-5
MASKED = -(2.0**127)


def at(per_batch, batch, k):
    return batch * per_batch + (k + 1)


def build(nc, x, adj, columns, expert_columns, w_qkv, w_o, b_o, w_attn, w_fc1, w_fc2, w_next, b_next, out):
    BATCHES, TOKENS, D = x.shape
    EXPERTS, _, HID = w_fc1.shape
    HEADS = 4
    DH = D // HEADS
    QT = TOKENS // P
    DC = D // P
    HC = HID // P
    HALF = HC // 2
    PAIRS = HEADS // 2
    TILES = HEADS * QT
    SCALE = DH ** -0.5
    STEPS = BATCHES

    with ExitStack() as ctx:
        def sb(name, shape, dt=F32):
            return ctx.enter_context(nc.sbuf_tensor(name, shape, dt))

        def bank(name):
            return ctx.enter_context(nc.psum_tensor(name, [P, 512], F32))

        def sem(name):
            return ctx.enter_context(nc.semaphore(name))

        ident = sb("ident", [P, P])
        minus_half = sb("minus_half", [P, QT])
        cols = sb("cols", [P, columns.shape[1]])
        g_col = cols[:, 0:DC]
        b_col = cols[:, DC:2 * DC]
        battn_col = cols[:, 2 * DC:3 * DC]
        expert_cols = sb("expert_cols", [P, HC + DC])
        bfc1_col = expert_cols[:, 0:HC]
        bfc2_col = expert_cols[:, HC:HC + DC]
        bo_rows = sb("bo_rows", [P, D])
        bnext_rows = sb("bnext_rows", [P, D])
        wqkv_hi = sb("wqkv_hi", [P, DC, 3 * D], F32R)
        wqkv_lo = sb("wqkv_lo", [P, DC, 3 * D], F32R)
        wsq_hi = sb("wsq_hi", [P, 3, DC, D], F32R)
        wsq_lo = sb("wsq_lo", [P, 3, DC, D], F32R)
        W_O, W_ATTN, W_NEXT = 0, 1, 2
        fc1_hi = sb("fc1_hi", [P, DC, HID], F32R)
        fc1_lo = sb("fc1_lo", [P, DC, HID], F32R)
        fc2_hi = sb("fc2_hi", [P, HC, D], F32R)
        fc2_lo = sb("fc2_lo", [P, HC, D], F32R)
        w_raw = sb("w_raw", [P, DC * HID])

        x_in = sb("x_in", [P, 2, QT, D])
        adj_words = sb("adj_words", [P, QT, TOKENS // 4], U32)
        adj_u8 = adj_words[:].bitcast(U8)
        mask = sb("mask", [P, QT, TOKENS], BF16)
        normed = sb("normed", [P, QT, D])
        xT_hi = sb("xT_hi", [P, DC, TOKENS], F32R)
        xT_lo = sb("xT_lo", [P, DC, TOKENS], F32R)
        qk_hi = sb("qk_hi", [P, 2 * PAIRS, TOKENS], F32R)
        qk_lo = sb("qk_lo", [P, 2 * PAIRS, TOKENS], F32R)
        v_cat = sb("v_cat", [P, QT, HEADS, 2 * DH], F32R)
        probs = sb("probs", [P, 4, TOKENS])
        shift = sb("shift", [P, 4])
        total = sb("total", [P, 4])
        inv_total = sb("inv_total", [P, 4])
        pT_hi = sb("pT_hi", [P, QT, TOKENS], F32R)
        pT_lo = sb("pT_lo", [P, QT, TOKENS], F32R)
        o_f32 = sb("o_f32", [P, TOKENS])
        oT_hi = sb("oT_hi", [P, PAIRS, TOKENS], F32R)
        oT_lo = sb("oT_lo", [P, PAIRS, TOKENS], F32R)

        x1 = sb("x1", [P, QT, D])
        y = sb("y", [P, QT, D])
        stats = sb("stats", [P, 3, QT, 6])
        moments = sb("moments", [P, 3, QT, 2])
        var_eps = sb("var_eps", [P, 3, QT])
        rstd = sb("rstd", [P, 3, QT])
        LN1, LN2, LN3 = 0, 1, 2
        nT_hi = sb("nT_hi", [P, DC, TOKENS], F32R)
        nT_lo = sb("nT_lo", [P, DC, TOKENS], F32R)
        whole = sb("whole", [P, DC * TOKENS])
        whole_T = whole[:, :].rearrange("p (c t) -> p c t", c=DC)
        whole_rows = whole[:, :].rearrange("p (t d) -> p t d", t=QT)
        aT_hi = sb("aT_hi", [P, DC, TOKENS], F32R)
        aT_lo = sb("aT_lo", [P, DC, TOKENS], F32R)
        hid = sb("hid", [P, HALF, TOKENS])
        yT = hid[:, 0:DC, :]
        h_hi = sb("h_hi", [P, HALF, TOKENS], F32R)
        h_lo = sb("h_lo", [P, HALF, TOKENS], F32R)

        score_ps = [bank(f"score_ps{i}") for i in range(3)]
        pT_ps = [bank(f"pT_ps{i}") for i in range(2)]
        o_ps = bank("o_ps")
        work_ps = [bank(f"work_ps{i}") for i in range(2)]

        consts_in = sem("consts_in")
        small_in = sem("small_in")
        consts_made = sem("consts_made")
        pool_made = sem("pool_made")
        wqkv_split = sem("wqkv_split")
        wsq_split = sem("wsq_split")
        x_in_dma = sem("x_in_dma")
        adj_in_dma = sem("adj_in_dma")
        wraw_dma = sem("wraw_dma")
        ecols_dma = sem("ecols_dma")
        w_hi_done = sem("w_hi_done")
        w_lo_done = sem("w_lo_done")
        rows_moved = sem("rows_moved")
        mask_done = sem("mask_done")
        stats_done = [sem(f"stats_done{i}") for i in range(3)]
        moments_done = [sem(f"moments_done{i}") for i in range(3)]
        eps_done = [sem(f"eps_done{i}") for i in range(3)]
        rstd_done = [sem(f"rstd_done{i}") for i in range(3)]
        xn_done = sem("xn_done")
        xbo_done = sem("xbo_done")
        y_done = sem("y_done")
        n_done = sem("n_done")
        xT_ready = sem("xT_ready")
        qk_ready = sem("qk_ready")
        v_ready = sem("v_ready")
        scores_ready = sem("scores_ready")
        pT_ready = sem("pT_ready")
        o_ready = sem("o_ready")
        wo_ready = sem("wo_ready")
        yT_ready = sem("yT_ready")
        nT_ready = sem("nT_ready")
        a_ready = sem("a_ready")
        fc1_ready = sem("fc1_ready")
        fc2_ready = sem("fc2_ready")
        next_ready = sem("next_ready")
        xT_hi_done = sem("xT_hi_done")
        qk_hi_done = sem("qk_hi_done")
        v_hi_done = sem("v_hi_done")
        exp_done = sem("exp_done")
        pT_hi_done = sem("pT_hi_done")
        o_second_taken = sem("o_second_taken")
        o_hi_done = sem("o_hi_done")
        yT_done = sem("yT_done")
        nT_hi_done = sem("nT_hi_done")
        a_hi_done = sem("a_hi_done")
        fc1_taken = sem("fc1_taken")
        gelu_done = sem("gelu_done")
        h_hi_done = sem("h_hi_done")
        fc2a_taken = sem("fc2a_taken")
        y2_hi_done = sem("y2_hi_done")
        zgelu_done = sem("zgelu_done")
        xT_lo_done = sem("xT_lo_done")
        qk_lo_done = sem("qk_lo_done")
        v_lo_done = sem("v_lo_done")
        masked_done = sem("masked_done")
        inv_done = sem("inv_done")
        probs_done = sem("probs_done")
        pT_lo_done = sem("pT_lo_done")
        o_added = sem("o_added")
        o_lo_done = sem("o_lo_done")
        x1_done = sem("x1_done")
        n_whole_done = sem("n_whole_done")
        a_whole_done = sem("a_whole_done")
        h_lo_dve = sem("h_lo_dve")
        y2_done = sem("y2_done")
        y2_lo_done = sem("y2_lo_done")
        z_done = sem("z_done")
        out_done = sem("out_done")
        nT_lo_done = sem("nT_lo_done")
        a_lo_done = sem("a_lo_done")
        h_lo_pool = sem("h_lo_pool")

        x_d = x.rearrange("b (t p) d -> b p t d", p=P)
        adj_d = adj.rearrange("b (t p) k -> b p t k", p=P)
        out_d = out.rearrange("b (t p) d -> b p t d", p=P)
        fc1_d = w_fc1.rearrange("e (c p) h -> e p c h", p=P)
        fc2_d = w_fc2.rearrange("e (c p) d -> e p c d", p=P)
        w_raw_fc1 = w_raw[:, :].rearrange("p (c h) -> p c h", c=DC)
        w_raw_fc2 = w_raw[:, :].rearrange("p (c d) -> p c d", c=HC)
        w_raw_qkv = w_raw[:, 0:DC * 3 * D].rearrange("p (c n) -> p c n", c=DC)
        w_raw_sq = hid[:, :, :].rearrange("p a b -> p (a b)")[:, 0:3 * DC * D].rearrange(
            "p (w c n) -> p w c n", w=3, c=DC)

        def f32(ap):
            return ap.bitcast(F32)

        dve_passed = sem("dve_passed")
        pool_passed = sem("pool_passed")
        sp_passed = sem("sp_passed")

        def wait_alone(engine, semaphore, value, passed):
            engine.wait_ge(semaphore, value)
            engine.sem_inc(passed, 1)

        block = ctx.enter_context(nc.Block())

        @block.sync
        def _(sp):
            sp.dma_start(w_raw_qkv, w_qkv.rearrange("(c p) n -> p c n", p=P)).then_inc(consts_in, 16)
            sp.dma_start(x_in[:, 0], x_d[0]).then_inc(x_in_dma, 16)
            for w, src in ((W_O, w_o), (W_ATTN, w_attn), (W_NEXT, w_next)):
                sp.dma_start(w_raw_sq[:, w], src.rearrange("(c p) n -> p c n", p=P)).then_inc(consts_in, 16)
            sp.dma_start(adj_words[:], adj_d[0]).then_inc(adj_in_dma, 16)
            sp.dma_start(cols[:], columns).then_inc(small_in, 16)
            sp.dma_start(bo_rows[:], b_o.partition_broadcast(P)).then_inc(small_in, 16)
            sp.dma_start(bnext_rows[:], b_next.partition_broadcast(P)).then_inc(small_in, 16)
            sp.dma_start(minus_half[0:1, :], b_next[0:QT].unsqueeze(0)).then_inc(rows_moved, 16)

            def step(n, attention=True, ffn=True, more=True, odd=None):
                if more:
                    if ffn:
                        wait_alone(sp, x1_done, at(2, n - 1, 1), sp_passed)
                    else:
                        sp.wait_ge(stats_done[LN1], at(QT, n, 0))
                    sp.dma_start(x_in[:, 1 - odd], x_d[n + 1]).then_inc(x_in_dma, 16)
                    wait_alone(sp, mask_done, at(QT, n, QT - 1), sp_passed)
                    sp.dma_start(adj_words[:], adj_d[n + 1]).then_inc(adj_in_dma, 16)

            def load_weights(e, first=False):
                if first:
                    sp.wait_ge(wqkv_split, 2)
                else:
                    wait_alone(sp, w_lo_done, at(2, e - 1, 1), sp_passed)
                sp.dma_start(w_raw_fc1, fc1_d[e]).then_inc(wraw_dma, 16)
                wait_alone(sp, w_hi_done, at(2, e, 0), sp_passed)
                sp.dma_start(expert_cols[:], expert_columns[e]).then_inc(ecols_dma, 16)
                wait_alone(sp, w_lo_done, at(2, e, 0), sp_passed)
                sp.dma_start(w_raw_fc2, fc2_d[e]).then_inc(wraw_dma, 16)

            def store(b):
                wait_alone(sp, out_done, at(1, b, 0), sp_passed)
                sp.dma_start(out_d[b], whole_rows).then_inc(rows_moved, 16)

            step(0, ffn=False, odd=0)
            load_weights(0, first=True)
            with sp.Fori(0, EXPERTS - 1) as e:
                step(2 * e + 1, odd=1)
                store(2 * e)
                step(2 * e + 2, odd=0)
                load_weights(e + 1)
                store(2 * e + 1)
            store(STEPS - 2)
            store(STEPS - 1)
            sp.wait_ge(rows_moved, 16 * (BATCHES + 1))

        @block.tensor
        def _(pe):
            mm = nc.tensor.matmul

            def split_product(ps, lhs, rhs, blocks):
                passes = [(a, b, c) for c in range(blocks) for a, b in ((0, 0), (0, 1), (1, 0))]
                for i, (a, b, c) in enumerate(passes):
                    last = mm(ps, lhs[a](c), rhs[b](c), start=(i == 0), stop=(i == len(passes) - 1))
                return last

            def both(hi, lo, pick):
                return (lambda c: pick(hi, c)), (lambda c: pick(lo, c))

            held = [None, None]
            turn = [0]

            def work_bank(taken, value):
                i = turn[0] % 2
                turn[0] += 1
                if held[i] is not None:
                    pe.wait_ge(*held[i])
                held[i] = (taken, value)
                return work_ps[i]

            def transposes(src, c, ready, taken, value):
                ps = work_bank(taken, value)
                for t in range(QT):
                    last = nc.tensor.transpose(ps[:, t * P:(t + 1) * P], src[:, t, c * P:(c + 1) * P], ident[:])
                last.then_inc(ready, 1)

            def x_transposes(b, c):
                if c == 0:
                    pe.wait_ge(xn_done, at(1, b, 0))
                transposes(normed, c, xT_ready, xT_lo_done, at(DC, b, c))

            def qk_products(b, j):
                if j == 0:
                    pe.wait_ge(xT_lo_done, at(DC, b, DC - 1))
                col = (j % 2) * D + (j // 2) * P
                ps = work_bank(qk_lo_done, at(2 * PAIRS, b, j))
                split_product(ps[:], both(wqkv_hi, wqkv_lo, lambda w, c: w[:, c, col:col + P]),
                              both(xT_hi, xT_lo, lambda w, c: w[:, c, :]), DC).then_inc(qk_ready, 1)

            def v_products(b, u):
                ps = work_bank(v_lo_done, at(2, b, u))
                for i in range(2):
                    t = 2 * u + i
                    last = split_product(ps[:, i * D:(i + 1) * D],
                                         both(xT_hi, xT_lo, lambda w, c: w[:, c, t * P:(t + 1) * P]),
                                         both(wqkv_hi, wqkv_lo, lambda w, c: w[:, c, 2 * D:3 * D]), DC)
                last.then_inc(v_ready, 1)

            def scores(n, k, first):
                h, t = divmod(k, QT)
                pair, r = divmod(h, 2)
                if t == 0 and r == 0:
                    pe.wait_ge(qk_lo_done, at(2 * PAIRS, n, 2 * pair + 1))
                if k >= 3:
                    pe.wait_ge(masked_done, at(TILES, n, k - 3))
                elif not first:
                    pe.wait_ge(masked_done, at(TILES, n - 1, TILES + k - 3))
                rows = slice(DH * r, DH * (r + 1))
                ps = score_ps[k % 3]
                split_product(ps[:], both(qk_hi, qk_lo, lambda w, c: w[rows, 2 * pair, t * P:(t + 1) * P]),
                              both(qk_hi, qk_lo, lambda w, c: w[rows, 2 * pair + 1, :]), 1).then_inc(scores_ready, 1)

            def prob_transposes(n, k, first):
                pe.wait_ge(probs_done, at(TILES, n, k))
                if k >= 2:
                    pe.wait_ge(pT_lo_done, at(TILES, n, k - 2))
                elif not first:
                    pe.wait_ge(pT_lo_done, at(TILES, n - 1, TILES + k - 2))
                ps = pT_ps[k % 2]
                for c in range(QT):
                    last = nc.tensor.transpose(ps[:, c * P:(c + 1) * P], probs[:, k % 4, c * P:(c + 1) * P], ident[:])
                last.then_inc(pT_ready, 1)

            def values(n, h, first):
                if h == 0:
                    pe.wait_ge(v_lo_done, at(2, n, 1))
                pe.wait_ge(pT_lo_done, at(TILES, n, QT * h + QT - 1))
                if h > 0:
                    pe.wait_ge(o_added, at(HEADS, n, h - 1))
                elif not first:
                    pe.wait_ge(o_added, at(HEADS, n - 1, HEADS - 1))
                for c in range(QT):
                    mm(o_ps[:], v_cat[:, c, h, :], pT_hi[:, c, :], start=(c == 0), stop=False)
                    last = mm(o_ps[:], v_cat[:, c, h, :], pT_lo[:, c, :], start=False, stop=(c == QT - 1))
                last.then_inc(o_ready, 1)

            def row_products(b, u, lhs_hi, lhs_lo, w, ready, taken):
                ps = work_bank(taken, at(2, b, u))
                for i in range(2):
                    t = 2 * u + i
                    last = split_product(ps[:, i * D:(i + 1) * D],
                                         both(lhs_hi, lhs_lo, lambda a, c: a[:, c, t * P:(t + 1) * P]),
                                         both(wsq_hi, wsq_lo, lambda a, c: a[:, w, c, :]), DC)
                last.then_inc(ready, 1)

            def attn_products(b, c_out):
                if c_out == 0:
                    pe.wait_ge(nT_lo_done, at(DC, b, DC - 1))
                ps = work_bank(a_whole_done, at(DC, b, c_out))
                split_product(ps[:], both(wsq_hi, wsq_lo, lambda w, c: w[:, W_ATTN, c, c_out * P:(c_out + 1) * P]),
                              both(nT_hi, nT_lo, lambda w, c: w[:, c, :]), DC).then_inc(a_ready, 1)

            def fc1_products(b, j):
                if j == 0:
                    pe.wait_ge(a_lo_done, at(DC, b, DC - 1))
                ps = work_bank(fc1_taken, at(HC, b, j))
                split_product(ps[:], both(fc1_hi, fc1_lo, lambda w, c: w[:, c, j * P:(j + 1) * P]),
                              both(aT_hi, aT_lo, lambda w, c: w[:, c, :]), DC).then_inc(fc1_ready, 1)

            def fc2_products(b, half, c_out):
                if c_out == 0:
                    pe.wait_ge(h_lo_dve, at(2, b, half))
                    pe.wait_ge(h_lo_pool, at(2, b, half))
                taken = y2_done if half else fc2a_taken
                ps = work_bank(taken, at(DC, b, c_out))
                split_product(ps[:], both(fc2_hi, fc2_lo, lambda w, c: w[:, half * HALF + c, c_out * P:(c_out + 1) * P]),
                              both(h_hi, h_lo, lambda w, c: w[:, c, :]), HALF).then_inc(fc2_ready, 1)

            def ffn_piece(m, e, new_weights, k):
                if k == 0:
                    pe.wait_ge(y_done, at(1, m, 0))
                    for c in range(DC):
                        transposes(y, c, yT_ready, yT_done, at(DC, m, c))
                elif k == 1:
                    pe.wait_ge(n_done, at(1, m, 0))
                    for c in range(DC):
                        transposes(normed, c, nT_ready, n_whole_done, at(DC, m, c))
                elif k == 3:
                    for c in range(DC):
                        attn_products(m, c)
                elif 4 <= k <= 7:
                    if k == 4 and new_weights:
                        pe.wait_ge(w_lo_done, at(2, e, 0))
                    fc1_products(m, k - 4)
                elif 9 <= k <= 12:
                    if k == 9:
                        fc1_products(m, 4)
                    elif k == 10:
                        fc1_products(m, 5)
                    elif k == 11:
                        if new_weights:
                            pe.wait_ge(w_lo_done, at(2, e, 1))
                        fc2_products(m, 0, 0)
                        fc2_products(m, 0, 1)
                    else:
                        fc1_products(m, 6)
                        fc1_products(m, 7)
                elif k == 16:
                    fc2_products(m, 1, 0)
                    fc2_products(m, 1, 1)
                elif k == 17:
                    pe.wait_ge(y2_lo_done, at(DC, m, DC - 1))
                    for u in range(2):
                        row_products(m, u, nT_hi, nT_lo, W_NEXT, next_ready, z_done)

            def step(n, attention=True, ffn=True, more=True, e=None, new_weights=False):
                first = not ffn
                if attention:
                    held[0] = (v_lo_done, at(2, n, 0))
                    held[1] = (v_lo_done, at(2, n, 1))
                for k in range(TILES + 2):
                    if attention and k < TILES:
                        scores(n, k, first)
                    if attention and k >= 2:
                        if k % QT == 2 and k > 2:
                            values(n, k // QT - 1, first)
                        prob_transposes(n, k - 2, first)
                    if more and k in (14, 15):
                        x_transposes(n + 1, k - 14)
                    if ffn:
                        ffn_piece(n - 1, e, new_weights, k)
                if attention:
                    values(n, HEADS - 1, first)
                if more:
                    qk_products(n + 1, 0)
                    qk_products(n + 1, 1)
                if attention:
                    pe.wait_ge(o_lo_done, at(PAIRS, n, PAIRS - 1))
                    for u in range(2):
                        row_products(n, u, oT_hi, oT_lo, W_O, wo_ready, x1_done)
                if more:
                    qk_products(n + 1, 2)
                    qk_products(n + 1, 3)
                    for u in range(2):
                        v_products(n + 1, u)

            pe.wait_ge(consts_made, 2)
            for c in range(DC):
                x_transposes(0, c)
            pe.wait_ge(wqkv_split, 2)
            for j in range(2 * PAIRS):
                qk_products(0, j)
            for u in range(2):
                v_products(0, u)
            pe.wait_ge(wsq_split, 2)
            step(0, ffn=False)
            with pe.Fori(0, EXPERTS - 1) as e:
                step(2 * e + 1, e=e, new_weights=True)
                step(2 * e + 2)
            step(STEPS - 1, e=EXPERTS - 1, new_weights=True, more=False)
            step(STEPS, attention=False, more=False)

        @block.scalar
        def _(act):
            A = nc.scalar.activation

            def x_hi(b, c):
                act.wait_ge(xT_ready, at(DC, b, c))
                A(xT_hi[:, c, :], work_ps[c % 2][:], ACT.Copy).then_inc(xT_hi_done, 1)

            def qk_part(b, j):
                act.wait_ge(qk_ready, at(2 * PAIRS, b, j))
                A(qk_hi[:, j, :], work_ps[j % 2][:], ACT.Copy).then_inc(qk_hi_done, 1)

            def v_part(b, u):
                act.wait_ge(v_ready, at(2, b, u))
                A(v_cat[:, 2 * u:2 * u + 2, :, 0:DH],
                  work_ps[u % 2][:].rearrange("p (t h d) -> p t h d", t=2, h=HEADS), ACT.Copy).then_inc(v_hi_done, 1)

            def exponentials(n, k):
                act.wait_ge(masked_done, at(TILES, n, k))
                A(probs[:, k % 4, :], probs[:, k % 4, :], ACT.Exp, bias=shift[:, k % 4:k % 4 + 1], scale=-1.0,
                  accum_out=total[:, k % 4:k % 4 + 1]).then_inc(exp_done, 1)

            def prob_hi(n, k, first):
                h, t = divmod(k, QT)
                act.wait_ge(pT_ready, at(TILES, n, k))
                if t == 0 and h > 0:
                    act.wait_ge(o_ready, at(HEADS, n, h - 1))
                elif t == 0 and not first:
                    act.wait_ge(o_ready, at(HEADS, n - 1, HEADS - 1))
                A(pT_hi[:, :, t * P:(t + 1) * P], pT_ps[k % 2][:].rearrange("p (c q) -> p c q", c=QT),
                  ACT.Copy).then_inc(pT_hi_done, 1)

            def take_second_half(n, h, first):
                pair, r = divmod(h, 2)
                act.wait_ge(o_ready, at(HEADS, n, h))
                if r == 0 and pair > 0:
                    act.wait_ge(o_lo_done, at(PAIRS, n, pair - 1))
                elif r == 0 and not first:
                    act.wait_ge(o_lo_done, at(PAIRS, n - 1, PAIRS - 1))
                A(o_f32[DH * r:DH * (r + 1), :], o_ps[DH:2 * DH, :], ACT.Copy).then_inc(o_second_taken, 1)

            def o_hi(n, pair, first):
                act.wait_ge(o_added, at(HEADS, n, 2 * pair + 1))
                if pair == 0 and not first:
                    act.wait_ge(wo_ready, at(2, n - 1, 1))
                A(oT_hi[:, pair, :], o_f32[:], ACT.Copy).then_inc(o_hi_done, 1)

            def ffn_piece(m, e, new_weights, k):
                if k == 0:
                    for c in range(DC):
                        act.wait_ge(yT_ready, at(DC, m, c))
                        A(yT[:, c, :], work_ps[c % 2][:], ACT.Identity,
                          bias=battn_col[:, c:c + 1]).then_inc(yT_done, 1)
                elif k == 1:
                    for c in range(DC):
                        act.wait_ge(nT_ready, at(DC, m, c))
                        A(nT_hi[:, c, :], work_ps[c % 2][:], ACT.Identity, bias=b_col[:, c:c + 1],
                          scale=g_col[:, c:c + 1]).then_inc(nT_hi_done, 1)
                elif k == 3:
                    for c in range(DC):
                        act.wait_ge(a_whole_done, at(DC, m, c))
                        A(aT_hi[:, c, :], whole_T[:, c, :], ACT.Copy).then_inc(a_hi_done, 1)
                elif k == 11:
                    fc2a_take(m, 0)
                    fc2a_take(m, 1)
                elif 4 <= k <= 7 or 9 <= k <= 12:
                    j = k - 4 if k <= 7 else (k - 5 if k < 11 else 6)
                    if j == 0 and new_weights:
                        act.wait_ge(ecols_dma, 16 * (e + 1))
                    if j == 0:
                        act.wait_ge(a_whole_done, at(DC, m, DC - 1))
                    if j == HALF:
                        act.wait_ge(h_lo_dve, at(2, m, 0))
                        act.wait_ge(h_lo_pool, at(2, m, 0))
                    fc1_take(m, j)
                    if k == 12:
                        j = 7
                        fc1_take(m, j)
                    if k in (7, 12):
                        half = k // 8
                        act.wait_ge(fc1_taken, at(HC, m, j))
                        A(hid[:], hid[:], ACT.Gelu).then_inc(gelu_done, 1)
                        act.wait_ge(gelu_done, at(2, m, half))
                        if half:
                            act.wait_ge(fc2_ready, at(2 * DC, m, DC - 1))
                        A(h_hi[:], hid[:], ACT.Copy).then_inc(h_hi_done, 1)
                elif k == 16:
                    for c in range(DC):
                        act.wait_ge(y2_done, at(DC, m, c))
                        A(nT_hi[:, c, :], whole_T[:, c, :], ACT.Copy).then_inc(y2_hi_done, 1)
                elif k == 17:
                    act.wait_ge(z_done, at(2, m, 1))
                    A(whole[:], whole[:], ACT.Gelu).then_inc(zgelu_done, 1)

            def fc1_take(m, j):
                act.wait_ge(fc1_ready, at(HC, m, j))
                A(hid[:, j % HALF, :], work_ps[j % 2][:], ACT.Identity,
                  bias=bfc1_col[:, j:j + 1]).then_inc(fc1_taken, 1)

            def fc2a_take(m, c):
                act.wait_ge(fc2_ready, at(2 * DC, m, c))
                if c == 0:
                    act.wait_ge(a_hi_done, at(DC, m, DC - 1))
                    act.wait_ge(a_lo_done, at(DC, m, DC - 1))
                A(whole_T[:, c, :], work_ps[c % 2][:], ACT.Identity,
                  bias=bfc2_col[:, c:c + 1]).then_inc(fc2a_taken, 1)

            def weight_hi(e, which, first=False):
                act.wait_ge(wraw_dma, 16 * (2 * e + which + 1))
                if not first:
                    b = 2 * e - 1
                    if which == 0:
                        act.wait_ge(fc1_ready, at(HC, b, HC - 1))
                    else:
                        act.wait_ge(fc2_ready, at(2 * DC, b, 2 * DC - 1))
                dst, src = (fc1_hi, w_raw_fc1) if which == 0 else (fc2_hi, w_raw_fc2)
                A(dst[:], src, ACT.Copy).then_inc(w_hi_done, 1)

            def step(n, attention=True, ffn=True, more=True, e=None, new_weights=False, new_e=None):
                first = not ffn
                for k in range(TILES + 2):
                    if attention and k < TILES:
                        exponentials(n, k)
                    if attention and k >= 2:
                        if k % QT == 2 and k > 2:
                            take_second_half(n, k // QT - 1, first)
                        if k == 11:
                            o_hi(n, 0, first)
                        prob_hi(n, k - 2, first)
                    if more and k in (14, 15):
                        x_hi(n + 1, k - 14)
                    if ffn:
                        ffn_piece(n - 1, e, new_weights, k)
                    if new_e is not None and k == 13:
                        weight_hi(new_e, 0, first=first)
                    if new_e is not None and k == 17:
                        weight_hi(new_e, 1, first=first)
                if attention:
                    take_second_half(n, HEADS - 1, first)
                if more:
                    qk_part(n + 1, 0)
                    qk_part(n + 1, 1)
                if attention:
                    o_hi(n, 1, first)
                if more:
                    qk_part(n + 1, 2)
                    qk_part(n + 1, 3)
                    v_part(n + 1, 0)
                    v_part(n + 1, 1)

            act.wait_ge(consts_in, 64)
            A(wqkv_hi[:], w_raw_qkv, ACT.Copy).then_inc(wqkv_split, 1)
            for c in range(DC):
                x_hi(0, c)
            A(wsq_hi[:], w_raw_sq, ACT.Copy).then_inc(wsq_split, 1)
            for j in range(2 * PAIRS):
                qk_part(0, j)
            for u in range(2):
                v_part(0, u)
            act.wait_ge(small_in, 16 * 3)
            act.wait_ge(wsq_split, 2)
            step(0, ffn=False, new_e=0)
            with act.Fori(0, EXPERTS - 1) as e:
                step(2 * e + 1, e=e, new_weights=True)
                step(2 * e + 2, new_e=e + 1)
            step(STEPS - 1, e=EXPERTS - 1, new_weights=True, more=False)
            step(STEPS, attention=False, more=False)

        @block.vector
        def _(dve):
            V = nc.vector

            def row_stats(b, which, src):
                for t in range(QT):
                    V.bn_stats(stats[:, which, t, :], src[:, t, :]).then_inc(stats_done[which], 1)
                wait_alone(dve, stats_done[which], at(QT, b, QT - 1), dve_passed)
                for t in range(QT):
                    last = V.bn_aggr(moments[:, which, t, :], stats[:, which, t, :])
                last.then_inc(moments_done[which], 1)

            def normalise(b, which, src, dst, done):
                dve.wait_ge(rstd_done[which], at(1, b, 0))
                for t in range(QT):
                    last = V.tensor_scalar(dst[:, t, :], src[:, t, :], moments[:, which, t, 0:1],
                                           rstd[:, which, t:t + 1], ALU.subtract, ALU.mult)
                last.then_inc(done, 1)

            def low_part(dst, src, hi, done):
                V.tensor_tensor(dst, src, f32(hi), ALU.subtract).then_inc(done, 1)

            def x_lo(b, c):
                dve.wait_ge(xT_hi_done, at(DC, b, c))
                low_part(xT_lo[:, c, :], work_ps[c % 2][:], xT_hi[:, c, :], xT_lo_done)

            def qk_part(b, j):
                dve.wait_ge(qk_hi_done, at(2 * PAIRS, b, j))
                low_part(qk_lo[:, j, :], work_ps[j % 2][:], qk_hi[:, j, :], qk_lo_done)

            def v_part(b, u):
                dve.wait_ge(v_hi_done, at(2, b, u))
                tt = slice(2 * u, 2 * u + 2)
                low_part(v_cat[:, tt, :, DH:2 * DH],
                         work_ps[u % 2][:].rearrange("p (t h d) -> p t h d", t=2, h=HEADS),
                         v_cat[:, tt, :, 0:DH], v_lo_done)

            def mask_and_max(n, k, first):
                t = k % QT
                if k < QT:
                    wait_alone(dve, mask_done, at(QT, n, t), dve_passed)
                if k >= 4:
                    wait_alone(dve, pT_ready, at(TILES, n, k - 4), dve_passed)
                elif not first:
                    wait_alone(dve, pT_ready, at(TILES, n - 1, TILES + k - 4), dve_passed)
                wait_alone(dve, scores_ready, at(TILES, n, k), dve_passed)
                V.tensor_tensor_reduce(out=probs[:, k % 4, :], in0=score_ps[k % 3][:], in1=mask[:, t, :],
                                       scale=-SCALE, scalar=3.0e38, op0=ALU.add, op1=ALU.min,
                                       accum_out=shift[:, k % 4:k % 4 + 1]).then_inc(masked_done, 1)

            def normalise_probs(n, k):
                dve.wait_ge(exp_done, at(TILES, n, k))
                V.reciprocal(inv_total[:, k % 4:k % 4 + 1], total[:, k % 4:k % 4 + 1]).then_inc(inv_done, 1)
                dve.wait_ge(inv_done, at(TILES, n, k))
                V.tensor_scalar(probs[:, k % 4, :], probs[:, k % 4, :], inv_total[:, k % 4:k % 4 + 1], None,
                                ALU.mult).then_inc(probs_done, 1)

            def prob_lo(n, k):
                t = k % QT
                dve.wait_ge(pT_hi_done, at(TILES, n, k))
                low_part(pT_lo[:, :, t * P:(t + 1) * P], pT_ps[k % 2][:].rearrange("p (c q) -> p c q", c=QT),
                         pT_hi[:, :, t * P:(t + 1) * P], pT_lo_done)

            def add_halves(n, h):
                rows = slice(DH * (h % 2), DH * (h % 2 + 1))
                dve.wait_ge(o_second_taken, at(HEADS, n, h))
                V.tensor_tensor(o_f32[rows, :], o_ps[0:DH, :], o_f32[rows, :], ALU.add).then_inc(o_added, 1)

            def o_lo(n, pair):
                dve.wait_ge(o_hi_done, at(PAIRS, n, pair))
                low_part(oT_lo[:, pair, :], o_f32[:], oT_hi[:, pair, :], o_lo_done)

            def residual(n, odd, u, ffn):
                if u == 0:
                    dve.wait_ge(xbo_done, at(1, n, 0))
                    if ffn:
                        dve.wait_ge(out_done, at(1, n - 1, 0))
                dve.wait_ge(wo_ready, at(2, n, u))
                tt = slice(2 * u, 2 * u + 2)
                V.tensor_tensor(x1[:, tt, :], work_ps[u % 2][:].rearrange("p (t d) -> p t d", t=2),
                                x_in[:, odd, tt, :], ALU.add).then_inc(x1_done, 1)

            def ffn_piece(m, k):
                if k == 0:
                    normalise(m, LN3, y, normed, n_done)
                elif k == 1:
                    for c in range(DC):
                        dve.wait_ge(nT_hi_done, at(DC, m, c))
                        if c == 0:
                            dve.wait_ge(rows_moved, at(1, m, 0) * 16)
                        V.tensor_scalar(whole_T[:, c, :], work_ps[c % 2][:], g_col[:, c:c + 1], b_col[:, c:c + 1],
                                        ALU.mult, ALU.add).then_inc(n_whole_done, 1)
                elif k == 3:
                    for c in range(DC):
                        dve.wait_ge(a_ready, at(DC, m, c))
                        dve.wait_ge(yT_done, at(DC, m, c))
                        dve.wait_ge(nT_lo_done, at(DC, m, c))
                        V.tensor_tensor(whole_T[:, c, :], work_ps[c % 2][:], yT[:, c, :],
                                        ALU.add).then_inc(a_whole_done, 1)
                elif k in (8, 13):
                    half = k // 13
                    dve.wait_ge(h_hi_done, at(2, m, half))
                    V.tensor_tensor(h_lo[:, 2:HALF, :], hid[:, 2:HALF, :], f32(h_hi[:, 2:HALF, :]),
                                    ALU.subtract).then_inc(h_lo_dve, 1)
                elif k == 16:
                    for c in range(DC):
                        dve.wait_ge(fc2_ready, at(2 * DC, m, DC + c))
                        dve.wait_ge(fc2a_taken, at(DC, m, c))
                        V.tensor_tensor(whole_T[:, c, :], work_ps[c % 2][:], whole_T[:, c, :],
                                        ALU.add).then_inc(y2_done, 1)
                    for c in range(DC):
                        dve.wait_ge(y2_hi_done, at(DC, m, c))
                        low_part(nT_lo[:, c, :], whole_T[:, c, :], nT_hi[:, c, :], y2_lo_done)
                elif k == 17:
                    for u in range(2):
                        dve.wait_ge(next_ready, at(2, m, u))
                        if u == 0:
                            dve.wait_ge(y2_lo_done, at(DC, m, DC - 1))
                        V.tensor_tensor(whole_rows[:, 2 * u:2 * u + 2, :],
                                        work_ps[u % 2][:].rearrange("p (t d) -> p t d", t=2),
                                        bnext_rows[:, :].unsqueeze(1).broadcast_to([P, 2, D]),
                                        ALU.add).then_inc(z_done, 1)

            def output_rows(m):
                dve.wait_ge(zgelu_done, at(1, m, 0))
                V.tensor_tensor(whole_rows, whole_rows, x1[:], ALU.add).then_inc(out_done, 1)

            def step(n, odd, attention=True, ffn=True, more=True):
                first = not ffn
                for k in range(TILES + 2):
                    if attention and k < TILES:
                        mask_and_max(n, k, first)
                    if attention and 1 <= k <= TILES:
                        normalise_probs(n, k - 1)
                    if attention and k >= 2:
                        if k % QT == 2 and k > 2:
                            add_halves(n, k // QT - 1)
                        if k == 11:
                            o_lo(n, 0)
                        prob_lo(n, k - 2)
                    if more and k == 10:
                        dve.wait_ge(x_in_dma, 16 * (n + 2))
                        if ffn:
                            dve.wait_ge(rstd_done[LN1], at(1, n, 0))
                        row_stats(n + 1, LN1, x_in[:, 1 - odd])
                    if more and k == 12:
                        if ffn:
                            dve.wait_ge(nT_ready, at(DC, n - 1, DC - 1))
                        else:
                            dve.wait_ge(xT_ready, at(DC, n, DC - 1))
                        normalise(n + 1, LN1, x_in[:, 1 - odd], normed, xn_done)
                    if more and k in (14, 15):
                        x_lo(n + 1, k - 14)
                    if ffn:
                        ffn_piece(n - 1, k)
                if attention:
                    add_halves(n, HEADS - 1)
                if more:
                    qk_part(n + 1, 0)
                    qk_part(n + 1, 1)
                if attention:
                    o_lo(n, 1)
                if ffn:
                    output_rows(n - 1)
                if attention:
                    residual(n, odd, 0, ffn)
                    residual(n, odd, 1, ffn)
                    dve.wait_ge(x1_done, at(2, n, 1))
                    row_stats(n, LN2, x1)
                if more:
                    qk_part(n + 1, 2)
                    qk_part(n + 1, 3)
                if attention:
                    normalise(n, LN2, x1, y, y_done)
                    dve.wait_ge(y_done, at(1, n, 0))
                    row_stats(n, LN3, y)
                if more:
                    v_part(n + 1, 0)
                    v_part(n + 1, 1)

            dve.wait_ge(x_in_dma, 16)
            row_stats(0, LN1, x_in[:, 0])
            dve.wait_ge(consts_in, 64)
            dve.wait_ge(wqkv_split, 1)
            V.tensor_tensor(wqkv_lo[:], w_raw_qkv, f32(wqkv_hi[:]), ALU.subtract).then_inc(wqkv_split, 1)
            normalise(0, LN1, x_in[:, 0], normed, xn_done)
            for c in range(DC):
                x_lo(0, c)
            dve.wait_ge(wsq_split, 1)
            V.tensor_tensor(wsq_lo[:], w_raw_sq, f32(wsq_hi[:]), ALU.subtract).then_inc(wsq_split, 1)
            for j in range(2 * PAIRS):
                qk_part(0, j)
            for u in range(2):
                v_part(0, u)
            dve.wait_ge(small_in, 16 * 3)
            step(0, 0, ffn=False)
            with dve.Fori(0, EXPERTS - 1) as e:
                step(2 * e + 1, 1)
                step(2 * e + 2, 0)
            step(STEPS - 1, 1, more=False)
            step(STEPS, 0, attention=False, more=False)

        @block.gpsimd
        def _(pool):
            G = nc.gpsimd

            def reciprocal_root(b, which):
                wait_alone(pool, moments_done[which], at(1, b, 0), pool_passed)
                G.tensor_scalar(var_eps[:, which, :], moments[:, which, :, 1], EPS, None,
                                ALU.add).then_inc(eps_done[which], 1)
                pool.wait_ge(eps_done[which], at(1, b, 0))
                G.tensor_tensor(rstd[:, which, :], var_eps[:, which, :], minus_half[:],
                                ALU.pow).then_inc(rstd_done[which], 1)

            def add_b_o(b, odd):
                pool.wait_ge(xn_done, at(1, b, 0))
                G.tensor_tensor(x_in[:, odd], x_in[:, odd], bo_rows[:, :].unsqueeze(1).broadcast_to([P, QT, D]),
                                ALU.add).then_inc(xbo_done, 1)

            def make_mask(b, t, first=False):
                if t == 0:
                    wait_alone(pool, adj_in_dma, 16 * (b + 1), pool_passed)
                if not first:
                    wait_alone(pool, masked_done, at(TILES, b - 1, TILES - QT + t), pool_passed)
                G.tensor_scalar(mask[:, t, :], adj_u8[:, t, :], -1.0, -MASKED, ALU.add,
                                ALU.mult).then_inc(mask_done, 1)

            def low_part(dst, src, hi, done):
                G.tensor_tensor(dst, src, f32(hi), ALU.subtract).then_inc(done, 1)

            def weight_lo(e, which):
                pool.wait_ge(w_hi_done, at(2, e, which))
                dst, src, hi = (fc1_lo, w_raw_fc1, fc1_hi) if which == 0 else (fc2_lo, w_raw_fc2, fc2_hi)
                low_part(dst[:], src, hi[:], w_lo_done)

            def ffn_piece(m, k):
                if k == 1:
                    for c in range(DC):
                        pool.wait_ge(n_whole_done, at(DC, m, c))
                        low_part(nT_lo[:, c, :], whole_T[:, c, :], nT_hi[:, c, :], nT_lo_done)
                elif k == 3:
                    for c in range(DC):
                        pool.wait_ge(a_hi_done, at(DC, m, c))
                        low_part(aT_lo[:, c, :], whole_T[:, c, :], aT_hi[:, c, :], a_lo_done)
                elif k in (8, 13):
                    half = k // 13
                    pool.wait_ge(h_hi_done, at(2, m, half))
                    low_part(h_lo[:, 0:2, :], hid[:, 0:2, :], h_hi[:, 0:2, :], h_lo_pool)

            def step(n, odd, attention=True, ffn=True, more=True, new_e=None):
                for k in range(TILES + 2):
                    if ffn:
                        ffn_piece(n - 1, k)
                    if more and k == 10:
                        reciprocal_root(n + 1, LN1)
                    if more and k == 12:
                        add_b_o(n + 1, 1 - odd)
                    if more and k >= 14:
                        make_mask(n + 1, k - 14)
                    if new_e is not None and k == 13:
                        weight_lo(new_e, 0)
                if attention:
                    reciprocal_root(n, LN2)
                    reciprocal_root(n, LN3)
                if new_e is not None:
                    weight_lo(new_e, 1)

            G.memset(ident[:], 1.0).then_inc(consts_made, 1)
            pool.wait_ge(rows_moved, 16)
            G.memset(minus_half[:], -0.5).then_inc(pool_made, 1)
            pool.wait_ge(consts_made, 1)
            G.affine_select(out=ident[:], in_=ident[:], compare_op=ALU.is_equal, fill=0.0, base=0,
                            pattern=[[-1, P]], channel_multiplier=1).then_inc(consts_made, 1)
            pool.wait_ge(pool_made, 1)
            reciprocal_root(0, LN1)
            for t in range(QT):
                make_mask(0, t, first=True)
            pool.wait_ge(small_in, 16 * 3)
            add_b_o(0, 0)
            step(0, 0, ffn=False, new_e=0)
            with pool.Fori(0, EXPERTS - 1) as e:
                step(2 * e + 1, 1)
                step(2 * e + 2, 0, new_e=e + 1)
            step(STEPS - 1, 1, more=False)
            step(STEPS, 0, attention=False, more=False)


def kernel(**inputs):
    import numpy as np
    import concourse.bacc as bacc
    from concourse.bass_utils import run_bass_kernel_spmd

    ins = {k: np.asarray(v) for k, v in inputs.items()}
    batches, tokens, d = ins["x"].shape
    experts = ins["L0_ffn_fc1_w"].shape[0]

    def by_expert(a):
        return np.ascontiguousarray(a.reshape(batches // experts, experts, *a.shape[1:]).swapaxes(0, 1)).reshape(a.shape)

    def as_columns(a):
        return a.reshape(-1, P).T

    vectors = ["L0_ffn_ln_g", "L0_ffn_ln_b", "L0_ffn_attn_b"]
    arrays = {
        "expert_columns": np.stack([np.concatenate([as_columns(b1), as_columns(b2)], axis=1)
                                    for b1, b2 in zip(ins["L0_ffn_fc1_b"], ins["L0_ffn_fc2_b"])]),
        "columns": np.concatenate([as_columns(ins[v]) for v in vectors], axis=1),
        "x": by_expert(ins["x"]),
        "adj": by_expert(ins["adj"]).view(np.uint32),
        "w_qkv": np.concatenate([ins["L0_gnn_Wq"], ins["L0_gnn_Wk"], ins["L0_gnn_Wv"]], axis=1),
        "w_o": ins["L0_gnn_Wo"],
        "b_o": ins["L0_gnn_bo"],
        "w_attn": ins["L0_ffn_attn_w"].T,
        "w_fc1": ins["L0_ffn_fc1_w"].transpose(0, 2, 1),
        "w_fc2": ins["L0_ffn_fc2_w"].transpose(0, 2, 1),
        "w_next": ins["L0_ffn_next_w"].T,
        "b_next": ins["L0_ffn_next_b"],
    }
    arrays = {k: np.ascontiguousarray(a) for k, a in arrays.items()}

    nc = bacc.Bacc("TRN2", target_bir_lowering=False, num_devices=1)
    args = {k: nc.dram_tensor(f"in_{k}", a.shape, mybir.dt.from_np(a.dtype), kind="ExternalInput").ap()
            for k, a in arrays.items()}
    out = nc.dram_tensor("out", (batches, tokens, d), F32, kind="ExternalOutput").ap()
    build(nc, out=out, **args)
    r = run_bass_kernel_spmd(nc, [{f"in_{k}": a for k, a in arrays.items()}], core_ids=[0])
    got = r.results[0]["out"]
    return np.ascontiguousarray(got.reshape(experts, batches // experts, tokens, d).swapaxes(0, 1)).reshape(batches, tokens, d)
```

```python
from contextlib import ExitStack

import concourse.bass as bass
from concourse import mybir
from concourse.alu_op_type import AluOpType as ALU

F32 = mybir.dt.float32
F32R = mybir.dt.float32r
BF16 = mybir.dt.bfloat16
U8 = mybir.dt.uint8
U32 = mybir.dt.uint32
ACT = mybir.ActivationFunctionType

P = 128
EPS = 1e-5
MASKED = -(2.0**127)


def at(per_batch, batch, k):
    return batch * per_batch + (k + 1)


def build(nc, x, adj, columns, expert_columns, w_qkv, w_o, b_o, w_attn, w_fc1, w_fc2, w_next, b_next, out):
    BATCHES, TOKENS, D = x.shape
    EXPERTS, _, HID = w_fc1.shape
    HEADS = 4
    DH = D // HEADS
    QT = TOKENS // P
    DC = D // P
    HC = HID // P
    HALF = HC // 2
    PAIRS = HEADS // 2
    TILES = HEADS * QT
    SCALE = DH ** -0.5
    SLOTS = TILES + 4
    LAST = BATCHES - 1

    with ExitStack() as ctx:
        def sb(name, shape, dt=F32):
            return ctx.enter_context(nc.sbuf_tensor(name, shape, dt))

        def bank(name):
            return ctx.enter_context(nc.psum_tensor(name, [P, 512], F32))

        def sem(name):
            return ctx.enter_context(nc.semaphore(name))

        ident = sb("ident", [P, P])
        minus_half = sb("minus_half", [P, QT])
        cols = sb("cols", [P, columns.shape[1]])
        g_col = cols[:, 0:DC]
        b_col = cols[:, DC:2 * DC]
        battn_col = cols[:, 2 * DC:3 * DC]
        expert_cols = sb("expert_cols", [P, HC + DC])
        bfc1_col = expert_cols[:, 0:HC]
        bfc2_col = expert_cols[:, HC:HC + DC]
        bo_rows = sb("bo_rows", [P, D])
        bnext_rows = sb("bnext_rows", [P, D])
        wqkv_hi = sb("wqkv_hi", [P, DC, 3 * D], F32R)
        wqkv_lo = sb("wqkv_lo", [P, DC, 3 * D], F32R)
        wsq_hi = sb("wsq_hi", [P, 3, DC, D], F32R)
        wsq_lo = sb("wsq_lo", [P, 3, DC, D], F32R)
        W_O, W_ATTN, W_NEXT = 0, 1, 2
        fc1_hi = sb("fc1_hi", [P, DC, HID], F32R)
        fc1_lo = sb("fc1_lo", [P, DC, HID], F32R)
        fc2_hi = sb("fc2_hi", [P, HC, D], F32R)
        fc2_lo = sb("fc2_lo", [P, HC, D], F32R)
        w_raw = sb("w_raw", [P, DC * HID])

        x_in = sb("x_in", [P, 2, QT, D])
        adj_words = sb("adj_words", [P, QT, TOKENS // 4], U32)
        adj_u8 = adj_words[:].bitcast(U8)
        mask = sb("mask", [P, QT, TOKENS], BF16)
        normed = sb("normed", [P, QT, D])
        xT_hi = sb("xT_hi", [P, DC, TOKENS], F32R)
        xT_lo = sb("xT_lo", [P, DC, TOKENS], F32R)
        qk_hi = sb("qk_hi", [P, 2 * PAIRS, TOKENS], F32R)
        qk_lo = sb("qk_lo", [P, 2 * PAIRS, TOKENS], F32R)
        v_cat = sb("v_cat", [P, QT, HEADS, 2 * DH], F32R)
        probs = sb("probs", [P, 4, TOKENS])
        shift = sb("shift", [P, 4])
        total = sb("total", [P, 4])
        inv_total = sb("inv_total", [P, 4])
        pT_hi = sb("pT_hi", [P, QT, TOKENS], F32R)
        pT_lo = sb("pT_lo", [P, QT, TOKENS], F32R)
        o_f32 = sb("o_f32", [P, TOKENS])
        oT_hi = sb("oT_hi", [P, PAIRS, TOKENS], F32R)
        oT_lo = sb("oT_lo", [P, PAIRS, TOKENS], F32R)

        x1 = sb("x1", [P, 2, QT, D])
        y = sb("y", [P, QT, D])
        stats = sb("stats", [P, 3, QT, 6])
        moments = sb("moments", [P, 3, QT, 2])
        var_eps = sb("var_eps", [P, 3, QT])
        rstd = sb("rstd", [P, 3, QT])
        LN1, LN2, LN3 = 0, 1, 2
        nT_hi = sb("nT_hi", [P, DC, TOKENS], F32R)
        nT_lo = sb("nT_lo", [P, DC, TOKENS], F32R)
        whole_T = sb("whole_T", [P, DC, TOKENS])
        rows_out = sb("rows_out", [P, QT, D])
        y2_T = rows_out[:, :, :].rearrange("p t d -> p (t d)").rearrange("p (c q) -> p c q", c=DC)
        aT_hi = sb("aT_hi", [P, DC, TOKENS], F32R)
        aT_lo = sb("aT_lo", [P, DC, TOKENS], F32R)
        hid = sb("hid", [P, HC, TOKENS])
        yT = hid[:, 0:DC, :]
        h_hi = sb("h_hi", [P, HALF, TOKENS], F32R)
        h_lo = sb("h_lo", [P, HALF, TOKENS], F32R)

        score_ps = [bank(f"score_ps{i}") for i in range(3)]
        pT_ps = [bank(f"pT_ps{i}") for i in range(2)]
        o_ps = bank("o_ps")
        work_ps = [bank(f"work_ps{i}") for i in range(2)]

        wqkv_in = sem("wqkv_in")
        wsq_in = sem("wsq_in")
        small_in = sem("small_in")
        consts_made = sem("consts_made")
        pool_made = sem("pool_made")
        wqkv_split = sem("wqkv_split")
        wsq_split = sem("wsq_split")
        x_in_dma = sem("x_in_dma")
        adj_in_dma = sem("adj_in_dma")
        wraw_dma = sem("wraw_dma")
        ecols_dma = sem("ecols_dma")
        w_hi_done = sem("w_hi_done")
        w_lo_done = sem("w_lo_done")
        rows_moved = sem("rows_moved")
        mask_done = sem("mask_done")
        stats_done = [sem(f"stats_done{i}") for i in range(3)]
        moments_done = [sem(f"moments_done{i}") for i in range(3)]
        eps_done = [sem(f"eps_done{i}") for i in range(3)]
        rstd_done = [sem(f"rstd_done{i}") for i in range(3)]
        xn_done = sem("xn_done")
        xbo_done = sem("xbo_done")
        y_done = sem("y_done")
        n_done = sem("n_done")
        xT_ready = sem("xT_ready")
        qk_ready = sem("qk_ready")
        v_ready = sem("v_ready")
        scores_ready = sem("scores_ready")
        pT_ready = sem("pT_ready")
        o_ready = sem("o_ready")
        wo_ready = sem("wo_ready")
        yT_ready = sem("yT_ready")
        nT_ready = sem("nT_ready")
        a_ready = sem("a_ready")
        fc1_ready = sem("fc1_ready")
        fc2_ready = sem("fc2_ready")
        next_ready = sem("next_ready")
        xT_hi_done = sem("xT_hi_done")
        qk_hi_done = sem("qk_hi_done")
        v_hi_done = sem("v_hi_done")
        exp_done = sem("exp_done")
        pT_hi_done = sem("pT_hi_done")
        o_second_taken = sem("o_second_taken")
        o_hi_done = sem("o_hi_done")
        yT_done = sem("yT_done")
        nT_hi_done = sem("nT_hi_done")
        a_hi_done = sem("a_hi_done")
        fc1_taken = sem("fc1_taken")
        gelu_done = sem("gelu_done")
        h_hi_done = sem("h_hi_done")
        fc2a_taken = sem("fc2a_taken")
        y2_hi_done = sem("y2_hi_done")
        zgelu_done = sem("zgelu_done")
        xT_lo_done = sem("xT_lo_done")
        qk_lo_done = sem("qk_lo_done")
        v_lo_done = sem("v_lo_done")
        masked_done = sem("masked_done")
        inv_done = sem("inv_done")
        probs_done = sem("probs_done")
        pT_lo_done = sem("pT_lo_done")
        o_added = sem("o_added")
        o_lo_done = sem("o_lo_done")
        x1_done = sem("x1_done")
        n_whole_done = sem("n_whole_done")
        a_whole_done = sem("a_whole_done")
        fc1_taken_dve = sem("fc1_taken_dve")
        a_lo_done = sem("a_lo_done")
        y2_done = sem("y2_done")
        y2_lo_done = sem("y2_lo_done")
        z_done = sem("z_done")
        out_done = sem("out_done")
        nT_lo_done = sem("nT_lo_done")
        h_lo_done = sem("h_lo_done")

        x_d = x.rearrange("b (t p) d -> b p t d", p=P)
        adj_d = adj.rearrange("b (t p) k -> b p t k", p=P)
        out_d = out.rearrange("b (t p) d -> b p t d", p=P)
        fc1_d = w_fc1.rearrange("e (c p) h -> e p c h", p=P)
        fc2_d = w_fc2.rearrange("e (c p) d -> e p c d", p=P)
        w_raw_fc1 = w_raw[:, :].rearrange("p (c h) -> p c h", c=DC)
        w_raw_fc2 = w_raw[:, :].rearrange("p (c d) -> p c d", c=HC)
        w_raw_qkv = w_raw[:, 0:DC * 3 * D].rearrange("p (c n) -> p c n", c=DC)
        w_raw_sq = hid[:, :, :].rearrange("p a b -> p (a b)")[:, 0:3 * DC * D].rearrange(
            "p (w c n) -> p w c n", w=3, c=DC)

        def f32(ap):
            return ap.bitcast(F32)

        dve_passed = sem("dve_passed")
        pool_passed = sem("pool_passed")
        sp_passed = sem("sp_passed")

        def wait_alone(engine, semaphore, value, passed):
            engine.wait_ge(semaphore, value)
            engine.sem_inc(passed, 1)

        block = ctx.enter_context(nc.Block())

        def running(edge, lag):
            return edge is None or 0 <= edge - lag <= LAST

        def had_one_before(edge, lag):
            return edge is None or edge - lag >= 1

        def tile_behind(k, d):
            return (0, k - d) if k >= d else (1, k - d + TILES)

        PRODUCTS = [
            [("fc1", 2, 2), ("qk", 2, 0)],
            [("next", 0, 3), ("next", 1, 3)],
            [("fc1", 3, 2), ("qk", 3, 0)],
            [("fc1", 4, 2), ("fc1", 5, 2)],
            [("fc1", 6, 2)],
            [("v", 0, 0), ("v", 1, 0)],
            [("wo", 0, 1), ("wo", 1, 1)],
            [("fc1", 7, 2)],
            [("fc2", 0, 2)],
            [("yT", 0, 1), ("yT", 1, 1), ("fc2", 1, 2)],
            [("nT", 0, 1), ("nT", 1, 1)],
            [("xT", 0, -1), ("xT", 1, -1)],
            [("attn", 0, 1), ("attn", 1, 1)],
            [("qk", 0, -1), ("fc2", 2, 2)],
            [("fc1", 0, 1), ("qk", 1, -1)],
            [("fc2", 3, 2), ("fc1", 1, 1)],
        ]
        TURNS = [(kind, j) for slot in PRODUCTS for kind, j, _ in slot]

        def bank_of(kind, j):
            return work_ps[TURNS.index((kind, j)) % 2]

        def score_bank(odd, k):
            order = (0, 2, 1) if odd else (0, 1, 2)
            return score_ps[order[1] if k == TILES - 1 else order[k % 3]]

        @block.sync
        def _(sp):
            def load_x(b, odd):
                wait_alone(sp, x1_done, at(2, b - 2, 1), sp_passed)
                sp.dma_start(x_in[:, odd], x_d[b]).then_inc(x_in_dma, 16)

            def load_adjacency(b):
                wait_alone(sp, mask_done, at(QT, b - 1, QT - 1), sp_passed)
                sp.dma_start(adj_words[:], adj_d[b]).then_inc(adj_in_dma, 16)

            def load_fc1(e, first):
                if first:
                    sp.wait_ge(wqkv_split, 2)
                else:
                    wait_alone(sp, w_lo_done, at(2, e - 1, 1), sp_passed)
                sp.dma_start(w_raw_fc1, fc1_d[e]).then_inc(wraw_dma, 16)

            def load_expert_columns(e, first):
                if not first:
                    wait_alone(sp, fc2a_taken, at(DC, 2 * e - 1, DC - 1), sp_passed)
                    wait_alone(sp, fc1_taken_dve, at(HALF, 2 * e - 1, HALF - 1), sp_passed)
                sp.dma_start(expert_cols[:], expert_columns[e]).then_inc(ecols_dma, 16)

            def load_fc2(e):
                wait_alone(sp, w_lo_done, at(2, e, 0), sp_passed)
                sp.dma_start(w_raw_fc2, fc2_d[e]).then_inc(wraw_dma, 16)

            def store(b):
                wait_alone(sp, out_done, at(1, b, 0), sp_passed)
                sp.dma_start(out_d[b], rows_out[:]).then_inc(rows_moved, 16)

            def step(n, odd, e, edge=None):
                if running(edge, -1):
                    load_adjacency(n + 1)
                if not odd and (edge is None or edge < 2 * (EXPERTS - 1) + 1):
                    load_fc1(e + 1, first=(edge == 0))
                if running(edge, 3):
                    store(n - 3)
                if running(edge, -1):
                    if edge == 0:
                        sp.wait_ge(stats_done[LN1], at(QT, 0, 0))
                        sp.dma_start(x_in[:, 1], x_d[1]).then_inc(x_in_dma, 16)
                    else:
                        load_x(n + 1, 1 - odd)
                if odd and (edge is None or edge <= LAST):
                    load_expert_columns(e, first=(edge == 1))
                    load_fc2(e)

            sp.dma_start(x_in[:, 0], x_d[0]).then_inc(x_in_dma, 16)
            sp.dma_start(w_raw_qkv, w_qkv.rearrange("(c p) n -> p c n", p=P)).then_inc(wqkv_in, 16)
            sp.dma_start(bo_rows[:], b_o.partition_broadcast(P)).then_inc(small_in, 16)
            sp.dma_start(adj_words[:], adj_d[0]).then_inc(adj_in_dma, 16)
            sp.dma_start(cols[:], columns).then_inc(small_in, 16)
            for w, src in ((W_O, w_o), (W_ATTN, w_attn), (W_NEXT, w_next)):
                sp.dma_start(w_raw_sq[:, w], src.rearrange("(c p) n -> p c n", p=P)).then_inc(wsq_in, 16)
            sp.dma_start(bnext_rows[:], b_next.partition_broadcast(P)).then_inc(rows_moved, 16)
            for n in range(0, 3):
                step(n, n % 2, (n - 1) // 2 if n % 2 else n // 2 - 1, edge=n)
            with sp.Fori(0, EXPERTS - 2) as i:
                step(2 * i + 3, 1, i + 1)
                step(2 * i + 4, 0, i + 1)
            for n in range(LAST, LAST + 4):
                step(n, n % 2, (n - 1) // 2 if n % 2 else n // 2 - 1, edge=n)
            sp.wait_ge(rows_moved, 16 * (BATCHES + 1))

        @block.tensor
        def _(pe):
            mm = nc.tensor.matmul

            def split_product(ps, lhs, rhs, blocks):
                passes = [(a, b, c) for c in range(blocks) for a, b in ((0, 0), (0, 1), (1, 0))]
                for i, (a, b, c) in enumerate(passes):
                    last = mm(ps, lhs[a](c), rhs[b](c), start=(i == 0), stop=(i == len(passes) - 1))
                return last

            def both(hi, lo, pick):
                return (lambda c: pick(hi, c)), (lambda c: pick(lo, c))

            def bank_read(kind, j, b):
                if kind == "fc1":
                    return (fc1_taken, at(HALF, b, j)) if j < HALF else (fc1_taken_dve, at(HALF, b, j - HALF))
                if kind == "fc2":
                    return (fc2a_taken, at(DC, b, j)) if j < DC else (y2_done, at(DC, b, j - DC))
                semaphore, count = {"xT": (xT_lo_done, DC), "qk": (qk_lo_done, 2 * PAIRS), "v": (v_lo_done, 2),
                                    "wo": (x1_done, 2), "yT": (yT_done, DC), "nT": (n_whole_done, DC),
                                    "attn": (a_whole_done, DC), "next": (z_done, 2)}[kind]
                return semaphore, at(count, b, j)

            def transposes(ps, src, c, ready):
                for t in range(QT):
                    last = nc.tensor.transpose(ps[:, t * P:(t + 1) * P], src[:, t, c * P:(c + 1) * P], ident[:])
                last.then_inc(ready, 1)

            def row_products(ps, u, lhs_hi, lhs_lo, rhs, ready):
                for i in range(2):
                    t = 2 * u + i
                    last = split_product(ps[:, i * D:(i + 1) * D],
                                         both(lhs_hi, lhs_lo, lambda a, c: a[:, c, t * P:(t + 1) * P]), rhs, DC)
                last.then_inc(ready, 1)

            def x_transposes(ps, b, c):
                if c == 0:
                    pe.wait_ge(xn_done, at(1, b, 0))
                transposes(ps, normed, c, xT_ready)

            def y_transposes(ps, b, c):
                if c == 0:
                    pe.wait_ge(y_done, at(1, b, 0))
                transposes(ps, y, c, yT_ready)

            def n_transposes(ps, b, c):
                if c == 0:
                    pe.wait_ge(n_done, at(1, b, 0))
                transposes(ps, y, c, nT_ready)

            def qk_products(ps, b, j):
                if j == 0:
                    pe.wait_ge(xT_lo_done, at(DC, b, DC - 1))
                col = (j % 2) * D + (j // 2) * P
                split_product(ps[:], both(wqkv_hi, wqkv_lo, lambda w, c: w[:, c, col:col + P]),
                              both(xT_hi, xT_lo, lambda w, c: w[:, c, :]), DC).then_inc(qk_ready, 1)

            def v_products(ps, b, u):
                row_products(ps, u, xT_hi, xT_lo, both(wqkv_hi, wqkv_lo, lambda w, c: w[:, c, 2 * D:3 * D]), v_ready)

            def wo_products(ps, b, u):
                if u == 0:
                    pe.wait_ge(o_lo_done, at(PAIRS, b, PAIRS - 1))
                row_products(ps, u, oT_hi, oT_lo, both(wsq_hi, wsq_lo, lambda w, c: w[:, W_O, c, :]), wo_ready)

            def next_products(ps, b, u):
                if u == 0:
                    pe.wait_ge(y2_lo_done, at(DC, b, DC - 1))
                row_products(ps, u, nT_hi, nT_lo, both(wsq_hi, wsq_lo, lambda w, c: w[:, W_NEXT, c, :]), next_ready)

            def attn_products(ps, b, c_out):
                if c_out == 0:
                    pe.wait_ge(nT_lo_done, at(DC, b, DC - 1))
                split_product(ps[:], both(wsq_hi, wsq_lo, lambda w, c: w[:, W_ATTN, c, c_out * P:(c_out + 1) * P]),
                              both(nT_hi, nT_lo, lambda w, c: w[:, c, :]), DC).then_inc(a_ready, 1)

            def fc1_products(ps, b, j):
                if j == 0:
                    pe.wait_ge(a_lo_done, at(DC, b, DC - 1))
                split_product(ps[:], both(fc1_hi, fc1_lo, lambda w, c: w[:, c, j * P:(j + 1) * P]),
                              both(aT_hi, aT_lo, lambda w, c: w[:, c, :]), DC).then_inc(fc1_ready, 1)

            def fc2_products(ps, b, j):
                half, c_out = divmod(j, DC)
                if c_out == 0:
                    pe.wait_ge(h_lo_done, at(2, b, half))
                split_product(ps[:], both(fc2_hi, fc2_lo, lambda w, c: w[:, half * HALF + c, c_out * P:(c_out + 1) * P]),
                              both(h_hi, h_lo, lambda w, c: w[:, c, :]), HALF).then_inc(fc2_ready, 1)

            product = {"xT": x_transposes, "yT": y_transposes, "nT": n_transposes, "qk": qk_products,
                       "v": v_products, "wo": wo_products, "next": next_products, "attn": attn_products,
                       "fc1": fc1_products, "fc2": fc2_products}

            def scores(n, odd, k, first):
                h, t = divmod(k, QT)
                pair, r = divmod(h, 2)
                if t == 0 and r == 0:
                    pe.wait_ge(qk_lo_done, at(2 * PAIRS, n, 2 * pair + 1))
                if k >= 3 or not first:
                    pe.wait_ge(masked_done, at(TILES, n, k - {0: 4, TILES - 1: 2}.get(k, 3)))
                rows = slice(DH * r, DH * (r + 1))
                ps = score_bank(odd, k)
                split_product(ps[:], both(qk_hi, qk_lo, lambda w, c: w[rows, 2 * pair, t * P:(t + 1) * P]),
                              both(qk_hi, qk_lo, lambda w, c: w[rows, 2 * pair + 1, :]), 1).then_inc(scores_ready, 1)

            def prob_transposes(b, k, first):
                pe.wait_ge(probs_done, at(TILES, b, k))
                if k >= 2 or not first:
                    pe.wait_ge(pT_lo_done, at(TILES, b, k - 2))
                ps = pT_ps[k % 2]
                for c in range(QT):
                    last = nc.tensor.transpose(ps[:, c * P:(c + 1) * P], probs[:, k % 4, c * P:(c + 1) * P], ident[:])
                last.then_inc(pT_ready, 1)

            def values(b, h, first):
                if h == 0:
                    pe.wait_ge(v_lo_done, at(2, b, 1))
                pe.wait_ge(pT_lo_done, at(TILES, b, QT * h + QT - 1))
                if h > 0 or not first:
                    pe.wait_ge(o_added, at(HEADS, b, h - 1))
                for c in range(QT):
                    mm(o_ps[:], v_cat[:, c, h, :], pT_hi[:, c, :], start=(c == 0), stop=False)
                    last = mm(o_ps[:], v_cat[:, c, h, :], pT_lo[:, c, :], start=False, stop=(c == QT - 1))
                last.then_inc(o_ready, 1)

            def step(n, odd, e, edge=None):
                if edge is None or edge == LAST:
                    for kind, j, lag in PRODUCTS[-1]:
                        held[TURNS.index((kind, j)) % 2] = bank_read(kind, j, n - 1 - lag)
                for k in range(TILES):
                    if running(edge, 0):
                        scores(n, odd, k, first=not had_one_before(edge, 0))
                    if k % QT == 0:
                        lag, last_tile = tile_behind(k, 5)
                        if running(edge, lag):
                            values(n - lag, last_tile // QT, first=not had_one_before(edge, lag))
                    lag, tile = tile_behind(k, 3)
                    if running(edge, lag):
                        prob_transposes(n - lag, tile, first=not had_one_before(edge, lag))
                    for kind, j, lag in PRODUCTS[k]:
                        if not running(edge, lag):
                            continue
                        if kind == "qk" and j == 0 and edge == -1:
                            pe.wait_ge(wqkv_split, 2)
                        if kind == "wo" and j == 0 and edge == 1:
                            pe.wait_ge(wsq_split, 2)
                        if kind == "fc1" and j == 0 and odd:
                            pe.wait_ge(w_lo_done, at(2, e, 0))
                        if kind == "fc2" and j == 0 and not odd:
                            pe.wait_ge(w_lo_done, at(2, e, 1))
                        i = TURNS.index((kind, j)) % 2
                        if held[i] is not None:
                            pe.wait_ge(*held[i])
                        held[i] = bank_read(kind, j, n - lag)
                        product[kind](bank_of(kind, j), n - lag, j)

            held = [None, None]
            pe.wait_ge(consts_made, 2)
            for n in range(-1, 3):
                step(n, n % 2, (n - 1) // 2 if n % 2 else n // 2 - 1, edge=n)
            with pe.Fori(0, EXPERTS - 2) as i:
                step(2 * i + 3, 1, i + 1)
                step(2 * i + 4, 0, i + 1)
            for n in range(LAST, LAST + 4):
                step(n, n % 2, (n - 1) // 2 if n % 2 else n // 2 - 1, edge=n)

        @block.scalar
        def _(act):
            A = nc.scalar.activation

            def x_hi(b, c):
                act.wait_ge(xT_ready, at(DC, b, c))
                A(xT_hi[:, c, :], bank_of("xT", c)[:], ACT.Copy).then_inc(xT_hi_done, 1)

            def qk_high(b, j):
                act.wait_ge(qk_ready, at(2 * PAIRS, b, j))
                A(qk_hi[:, j, :], bank_of("qk", j)[:], ACT.Copy).then_inc(qk_hi_done, 1)

            def v_high(b, u):
                act.wait_ge(v_ready, at(2, b, u))
                A(v_cat[:, 2 * u:2 * u + 2, :, 0:DH],
                  bank_of("v", u)[:].rearrange("p (t h d) -> p t h d", t=2, h=HEADS), ACT.Copy).then_inc(v_hi_done, 1)

            def exponentials(n, k):
                act.wait_ge(masked_done, at(TILES, n, k))
                A(probs[:, k % 4, :], probs[:, k % 4, :], ACT.Exp, bias=shift[:, k % 4:k % 4 + 1], scale=-1.0,
                  accum_out=total[:, k % 4:k % 4 + 1]).then_inc(exp_done, 1)

            def prob_hi(b, k, first):
                h, t = divmod(k, QT)
                act.wait_ge(pT_ready, at(TILES, b, k))
                if t == 0 and (h > 0 or not first):
                    act.wait_ge(o_ready, at(HEADS, b, h - 1))
                A(pT_hi[:, :, t * P:(t + 1) * P], pT_ps[k % 2][:].rearrange("p (c q) -> p c q", c=QT),
                  ACT.Copy).then_inc(pT_hi_done, 1)

            def take_second_half(b, h, first):
                pair, r = divmod(h, 2)
                act.wait_ge(o_ready, at(HEADS, b, h))
                if r == 0 and (pair > 0 or not first):
                    act.wait_ge(o_lo_done, at(PAIRS, b, pair - 1))
                A(o_f32[DH * r:DH * (r + 1), :], o_ps[DH:2 * DH, :], ACT.Copy).then_inc(o_second_taken, 1)

            def o_hi(b, pair):
                act.wait_ge(o_added, at(HEADS, b, 2 * pair + 1))
                A(oT_hi[:, pair, :], o_f32[:], ACT.Copy).then_inc(o_hi_done, 1)

            def y_take(m, c):
                act.wait_ge(yT_ready, at(DC, m, c))
                A(yT[:, c, :], bank_of("yT", c)[:], ACT.Identity, bias=battn_col[:, c:c + 1]).then_inc(yT_done, 1)

            def n_hi(m, c):
                act.wait_ge(nT_ready, at(DC, m, c))
                A(nT_hi[:, c, :], bank_of("nT", c)[:], ACT.Identity, bias=b_col[:, c:c + 1],
                  scale=g_col[:, c:c + 1]).then_inc(nT_hi_done, 1)

            def a_hi(m, c):
                act.wait_ge(a_whole_done, at(DC, m, c))
                A(aT_hi[:, c, :], whole_T[:, c, :], ACT.Copy).then_inc(a_hi_done, 1)

            def fc1_take(m, j):
                act.wait_ge(fc1_ready, at(HC, m, j))
                A(hid[:, j, :], bank_of("fc1", j)[:], ACT.Identity,
                  bias=bfc1_col[:, j:j + 1]).then_inc(fc1_taken, 1)

            def gelu(m, half):
                done = fc1_taken_dve if half else fc1_taken
                act.wait_ge(done, at(HALF, m, HALF - 1))
                rows = slice(half * HALF, (half + 1) * HALF)
                A(hid[:, rows, :], hid[:, rows, :], ACT.Gelu).then_inc(gelu_done, 1)

            def h_high(m, half):
                act.wait_ge(gelu_done, at(2, m, half))
                if half:
                    act.wait_ge(fc2_ready, at(2 * DC, m, DC - 1))
                A(h_hi[:], hid[:, half * HALF:(half + 1) * HALF, :], ACT.Copy).then_inc(h_hi_done, 1)

            def fc2a_take(m, c):
                if c == 0:
                    act.wait_ge(rows_moved, 16 * at(1, m, 0))
                act.wait_ge(fc2_ready, at(2 * DC, m, c))
                A(y2_T[:, c, :], bank_of("fc2", c)[:], ACT.Identity,
                  bias=bfc2_col[:, c:c + 1]).then_inc(fc2a_taken, 1)

            def y2_hi(m, c):
                act.wait_ge(y2_done, at(DC, m, c))
                A(nT_hi[:, c, :], y2_T[:, c, :], ACT.Copy).then_inc(y2_hi_done, 1)

            def z_gelu(b):
                act.wait_ge(z_done, at(2, b, 1))
                A(rows_out[:], rows_out[:], ACT.Gelu).then_inc(zgelu_done, 1)

            def weight_hi(e, which, first):
                act.wait_ge(wraw_dma, 16 * (2 * e + which + 1))
                if not first:
                    b = 2 * e - 1
                    if which == 0:
                        act.wait_ge(fc1_ready, at(HC, b, HC - 1))
                    else:
                        act.wait_ge(fc2_ready, at(2 * DC, b, 2 * DC - 1))
                dst, src = (fc1_hi, w_raw_fc1) if which == 0 else (fc2_hi, w_raw_fc2)
                A(dst[:], src, ACT.Copy).then_inc(w_hi_done, 1)

            def step(n, odd, e, edge=None):
                for k in range(TILES):
                    if running(edge, 0):
                        exponentials(n, k)
                    if k % QT == 0:
                        lag, last_tile = tile_behind(k, 5)
                        if running(edge, lag):
                            take_second_half(n - lag, last_tile // QT, first=not had_one_before(edge, lag))
                    lag, tile = tile_behind(k, 4)
                    if running(edge, lag):
                        prob_hi(n - lag, tile, first=not had_one_before(edge, lag))

                    if running(edge, -1):
                        if k == 11:
                            x_hi(n + 1, 0)
                            x_hi(n + 1, 1)
                        elif k == 13:
                            qk_high(n + 1, 0)
                    if running(edge, 0):
                        if k == 5:
                            v_high(n, 0)
                            v_high(n, 1)
                        elif k == 13:
                            o_hi(n, 0)
                    if running(edge, 1):
                        if k == 5:
                            o_hi(n - 1, 1)
                        elif k == 9:
                            y_take(n - 1, 0)
                            y_take(n - 1, 1)
                        elif k == 10:
                            n_hi(n - 1, 0)
                            n_hi(n - 1, 1)
                        elif k == 12:
                            a_hi(n - 1, 0)
                            a_hi(n - 1, 1)
                        elif k == 14:
                            if odd:
                                act.wait_ge(ecols_dma, 16 * (e + 1))
                            fc1_take(n - 1, 0)
                        elif k == 15:
                            fc1_take(n - 1, 1)
                    if running(edge, 2):
                        if k in (0, 2):
                            fc1_take(n - 2, 2 + k // 2)
                        elif k == 3:
                            if running(edge, 3):
                                z_gelu(n - 3)
                            gelu(n - 2, 0)
                        elif k == 4:
                            h_high(n - 2, 0)
                        elif k == 8:
                            gelu(n - 2, 1)
                            fc2a_take(n - 2, 0)
                        elif k == 9:
                            fc2a_take(n - 2, 1)
                        elif k == 10:
                            h_high(n - 2, 1)
                        elif k == 14:
                            y2_hi(n - 2, 0)
                    elif k == 3 and running(edge, 3):
                        z_gelu(n - 3)
                    if k == 0 and running(edge, 3):
                        y2_hi(n - 3, 1)
                    if running(edge, 0) and k in (0, 2):
                        qk_high(n, 2 + k // 2)
                    if running(edge, -1) and k == 14:
                        qk_high(n + 1, 1)
                    if odd and k == 8 and running(edge, 1):
                        weight_hi(e, 0, first=(edge == 1))
                    if not odd and k == 0 and running(edge, 2):
                        weight_hi(e, 1, first=(edge == 2))

            act.wait_ge(wqkv_in, 16)
            A(wqkv_hi[:], w_raw_qkv, ACT.Copy).then_inc(wqkv_split, 1)
            step(-1, 1, None, edge=-1)
            act.wait_ge(wsq_in, 16 * 3)
            A(wsq_hi[:], w_raw_sq, ACT.Copy).then_inc(wsq_split, 1)
            act.wait_ge(small_in, 16 * 2)
            for n in range(0, 3):
                step(n, n % 2, (n - 1) // 2 if n % 2 else n // 2 - 1, edge=n)
            with act.Fori(0, EXPERTS - 2) as i:
                step(2 * i + 3, 1, i + 1)
                step(2 * i + 4, 0, i + 1)
            for n in range(LAST, LAST + 4):
                step(n, n % 2, (n - 1) // 2 if n % 2 else n // 2 - 1, edge=n)

        @block.vector
        def _(dve):
            V = nc.vector

            def row_stats(b, which, src):
                for t in range(QT):
                    V.bn_stats(stats[:, which, t, :], src[:, t, :]).then_inc(stats_done[which], 1)
                wait_alone(dve, stats_done[which], at(QT, b, QT - 1), dve_passed)
                for t in range(QT):
                    last = V.bn_aggr(moments[:, which, t, :], stats[:, which, t, :])
                last.then_inc(moments_done[which], 1)

            def normalise(b, which, src, dst, done):
                dve.wait_ge(rstd_done[which], at(1, b, 0))
                for t in range(QT):
                    last = V.tensor_scalar(dst[:, t, :], src[:, t, :], moments[:, which, t, 0:1],
                                           rstd[:, which, t:t + 1], ALU.subtract, ALU.mult)
                last.then_inc(done, 1)

            def low_part(dst, src, hi, done):
                V.tensor_tensor(dst, src, f32(hi), ALU.subtract).then_inc(done, 1)

            def x_lo(b, c):
                dve.wait_ge(xT_hi_done, at(DC, b, c))
                low_part(xT_lo[:, c, :], bank_of("xT", c)[:], xT_hi[:, c, :], xT_lo_done)

            def qk_low(b, j):
                dve.wait_ge(qk_hi_done, at(2 * PAIRS, b, j))
                low_part(qk_lo[:, j, :], bank_of("qk", j)[:], qk_hi[:, j, :], qk_lo_done)

            def v_low(b, u):
                dve.wait_ge(v_hi_done, at(2, b, u))
                tt = slice(2 * u, 2 * u + 2)
                low_part(v_cat[:, tt, :, DH:2 * DH],
                         bank_of("v", u)[:].rearrange("p (t h d) -> p t h d", t=2, h=HEADS),
                         v_cat[:, tt, :, 0:DH], v_lo_done)

            def mask_and_max(n, odd, k, first):
                t = k % QT
                if k < QT:
                    wait_alone(dve, mask_done, at(QT, n, t), dve_passed)
                if k >= 4 or not first:
                    wait_alone(dve, pT_ready, at(TILES, n, k - 4), dve_passed)
                wait_alone(dve, scores_ready, at(TILES, n, k), dve_passed)
                V.tensor_tensor_reduce(out=probs[:, k % 4, :], in0=score_bank(odd, k)[:], in1=mask[:, t, :],
                                       scale=-SCALE, scalar=3.0e38, op0=ALU.add, op1=ALU.min,
                                       accum_out=shift[:, k % 4:k % 4 + 1]).then_inc(masked_done, 1)

            def normalise_probs(b, k):
                dve.wait_ge(exp_done, at(TILES, b, k))
                V.reciprocal(inv_total[:, k % 4:k % 4 + 1], total[:, k % 4:k % 4 + 1]).then_inc(inv_done, 1)
                dve.wait_ge(inv_done, at(TILES, b, k))
                V.tensor_scalar(probs[:, k % 4, :], probs[:, k % 4, :], inv_total[:, k % 4:k % 4 + 1], None,
                                ALU.mult).then_inc(probs_done, 1)

            def prob_lo(b, k):
                t = k % QT
                dve.wait_ge(pT_hi_done, at(TILES, b, k))
                low_part(pT_lo[:, :, t * P:(t + 1) * P], pT_ps[k % 2][:].rearrange("p (c q) -> p c q", c=QT),
                         pT_hi[:, :, t * P:(t + 1) * P], pT_lo_done)

            def add_halves(b, h):
                rows = slice(DH * (h % 2), DH * (h % 2 + 1))
                dve.wait_ge(o_second_taken, at(HEADS, b, h))
                V.tensor_tensor(o_f32[rows, :], o_ps[0:DH, :], o_f32[rows, :], ALU.add).then_inc(o_added, 1)

            def o_lo(b, pair):
                dve.wait_ge(o_hi_done, at(PAIRS, b, pair))
                low_part(oT_lo[:, pair, :], o_f32[:], oT_hi[:, pair, :], o_lo_done)

            def residual(b, odd, u, half_was_used):
                if u == 0:
                    dve.wait_ge(xbo_done, at(1, b, 0))
                    if half_was_used:
                        dve.wait_ge(out_done, at(1, b - 2, 0))
                dve.wait_ge(wo_ready, at(2, b, u))
                tt = slice(2 * u, 2 * u + 2)
                V.tensor_tensor(x1[:, odd, tt, :], bank_of("wo", u)[:].rearrange("p (t d) -> p t d", t=2),
                                x_in[:, odd, tt, :], ALU.add).then_inc(x1_done, 1)

            def n_whole(m, c):
                dve.wait_ge(nT_hi_done, at(DC, m, c))
                V.tensor_scalar(whole_T[:, c, :], bank_of("nT", c)[:], g_col[:, c:c + 1], b_col[:, c:c + 1],
                                ALU.mult, ALU.add).then_inc(n_whole_done, 1)

            def a_whole(m, c):
                dve.wait_ge(a_ready, at(DC, m, c))
                dve.wait_ge(yT_done, at(DC, m, c))
                dve.wait_ge(nT_lo_done, at(DC, m, c))
                V.tensor_tensor(whole_T[:, c, :], bank_of("attn", c)[:], yT[:, c, :],
                                ALU.add).then_inc(a_whole_done, 1)

            def a_lo(m, c):
                dve.wait_ge(a_hi_done, at(DC, m, c))
                low_part(aT_lo[:, c, :], whole_T[:, c, :], aT_hi[:, c, :], a_lo_done)

            def fc1_take(m, j):
                dve.wait_ge(fc1_ready, at(HC, m, j))
                V.tensor_scalar(hid[:, j, :], bank_of("fc1", j)[:], bfc1_col[:, j:j + 1], None,
                                ALU.add).then_inc(fc1_taken_dve, 1)

            def y2_whole(m, c):
                dve.wait_ge(fc2_ready, at(2 * DC, m, DC + c))
                dve.wait_ge(fc2a_taken, at(DC, m, c))
                V.tensor_tensor(y2_T[:, c, :], bank_of("fc2", DC + c)[:], y2_T[:, c, :],
                                ALU.add).then_inc(y2_done, 1)

            def y2_lo(m, c):
                dve.wait_ge(y2_hi_done, at(DC, m, c))
                low_part(nT_lo[:, c, :], y2_T[:, c, :], nT_hi[:, c, :], y2_lo_done)

            def z_take(b, u):
                dve.wait_ge(next_ready, at(2, b, u))
                V.tensor_tensor(rows_out[:, 2 * u:2 * u + 2, :],
                                bank_of("next", u)[:].rearrange("p (t d) -> p t d", t=2),
                                bnext_rows[:, :].unsqueeze(1).broadcast_to([P, 2, D]),
                                ALU.add).then_inc(z_done, 1)

            def step(n, odd, e, edge=None):
                for k in range(TILES):
                    if running(edge, 0):
                        mask_and_max(n, odd, k, first=not had_one_before(edge, 0))
                    lag, tile = tile_behind(k, 1)
                    if running(edge, lag):
                        normalise_probs(n - lag, tile)
                    if k % QT == 0:
                        lag, last_tile = tile_behind(k, 5)
                        if running(edge, lag):
                            add_halves(n - lag, last_tile // QT)
                    lag, tile = tile_behind(k, 4)
                    if running(edge, lag):
                        prob_lo(n - lag, tile)

                    if running(edge, -1):
                        if k == 9:
                            wait_alone(dve, x_in_dma, 16 * (n + 2), dve_passed)
                            if edge != -1:
                                wait_alone(dve, xn_done, at(1, n, 0), dve_passed)
                            row_stats(n + 1, LN1, x_in[:, 1 - odd])
                        elif k == 11:
                            if edge == -1:
                                dve.wait_ge(wqkv_in, 16)
                                dve.wait_ge(wqkv_split, 1)
                                V.tensor_tensor(wqkv_lo[:], w_raw_qkv, f32(wqkv_hi[:]),
                                                ALU.subtract).then_inc(wqkv_split, 1)
                            x_lo(n + 1, 0)
                            x_lo(n + 1, 1)
                        elif k == 13:
                            qk_low(n + 1, 0)
                    if running(edge, 0):
                        if k == 5:
                            v_low(n, 0)
                            v_low(n, 1)
                        elif k == 13:
                            o_lo(n, 0)
                    if running(edge, 1):
                        if k == 5:
                            o_lo(n - 1, 1)
                        elif k == 6:
                            residual(n - 1, 1 - odd, 0, running(edge, 3))
                            residual(n - 1, 1 - odd, 1, running(edge, 3))
                            wait_alone(dve, x1_done, at(2, n - 1, 1), dve_passed)
                            row_stats(n - 1, LN2, x1[:, 1 - odd])
                        elif k == 7:
                            normalise(n - 1, LN2, x1[:, 1 - odd], y, y_done)
                        elif k == 8:
                            wait_alone(dve, y_done, at(1, n - 1, 0), dve_passed)
                            row_stats(n - 1, LN3, y)
                        elif k == 9:
                            dve.wait_ge(yT_ready, at(DC, n - 1, DC - 1))
                            normalise(n - 1, LN3, y, y, n_done)
                        elif k == 10:
                            n_whole(n - 1, 0)
                            n_whole(n - 1, 1)
                        elif k == 12:
                            a_whole(n - 1, 0)
                            a_whole(n - 1, 1)
                            a_lo(n - 1, 0)
                            a_lo(n - 1, 1)
                    if running(edge, 2):
                        if k == 3:
                            if not odd:
                                dve.wait_ge(ecols_dma, 16 * (e + 1))
                            fc1_take(n - 2, 4)
                            fc1_take(n - 2, 5)
                        elif k == 4:
                            fc1_take(n - 2, 6)
                        elif k == 7:
                            fc1_take(n - 2, 7)
                        elif k == 13:
                            y2_whole(n - 2, 0)
                        elif k == 15:
                            y2_whole(n - 2, 1)
                    if running(edge, 3):
                        if k == 0:
                            y2_lo(n - 3, 0)
                            y2_lo(n - 3, 1)
                        elif k == 1:
                            z_take(n - 3, 0)
                            z_take(n - 3, 1)
                    if running(edge, 0) and k in (0, 2):
                        qk_low(n, 2 + k // 2)
                    if running(edge, -1) and k == 14:
                        qk_low(n + 1, 1)

            dve.wait_ge(x_in_dma, 16)
            step(-1, 1, None, edge=-1)
            dve.wait_ge(wsq_in, 16 * 3)
            dve.wait_ge(wsq_split, 1)
            V.tensor_tensor(wsq_lo[:], w_raw_sq, f32(wsq_hi[:]), ALU.subtract).then_inc(wsq_split, 1)
            dve.wait_ge(small_in, 16 * 2)
            for n in range(0, 3):
                step(n, n % 2, (n - 1) // 2 if n % 2 else n // 2 - 1, edge=n)
            with dve.Fori(0, EXPERTS - 2) as i:
                step(2 * i + 3, 1, i + 1)
                step(2 * i + 4, 0, i + 1)
            for n in range(LAST, LAST + 4):
                step(n, n % 2, (n - 1) // 2 if n % 2 else n // 2 - 1, edge=n)

        @block.gpsimd
        def _(pool):
            G = nc.gpsimd

            def reciprocal_root(b, which):
                wait_alone(pool, moments_done[which], at(1, b, 0), pool_passed)
                G.tensor_scalar(var_eps[:, which, :], moments[:, which, :, 1], EPS, None,
                                ALU.add).then_inc(eps_done[which], 1)
                pool.wait_ge(eps_done[which], at(1, b, 0))
                G.tensor_tensor(rstd[:, which, :], var_eps[:, which, :], minus_half[:],
                                ALU.pow).then_inc(rstd_done[which], 1)

            def normalise_x(b, odd, first):
                if not first:
                    wait_alone(pool, xT_ready, at(DC, b - 1, DC - 1), pool_passed)
                wait_alone(pool, rstd_done[LN1], at(1, b, 0), pool_passed)
                for t in range(QT):
                    last = G.tensor_scalar(normed[:, t, :], x_in[:, odd, t, :], moments[:, LN1, t, 0:1],
                                           rstd[:, LN1, t:t + 1], ALU.subtract, ALU.mult)
                last.then_inc(xn_done, 1)

            def add_b_o(b, odd):
                pool.wait_ge(xn_done, at(1, b, 0))
                G.tensor_tensor(x_in[:, odd], x_in[:, odd], bo_rows[:, :].unsqueeze(1).broadcast_to([P, QT, D]),
                                ALU.add).then_inc(xbo_done, 1)

            def make_mask(b, t, first):
                if t == 0:
                    wait_alone(pool, adj_in_dma, 16 * (b + 1), pool_passed)
                if not first:
                    wait_alone(pool, masked_done, at(TILES, b, t - QT), pool_passed)
                G.tensor_scalar(mask[:, t, :], adj_u8[:, t, :], -1.0, -MASKED, ALU.add,
                                ALU.mult).then_inc(mask_done, 1)

            def low_part(dst, src, hi, done):
                G.tensor_tensor(dst, src, f32(hi), ALU.subtract).then_inc(done, 1)

            def weight_lo(e, which):
                pool.wait_ge(w_hi_done, at(2, e, which))
                dst, src, hi = (fc1_lo, w_raw_fc1, fc1_hi) if which == 0 else (fc2_lo, w_raw_fc2, fc2_hi)
                low_part(dst[:], src, hi[:], w_lo_done)

            def h_low(m, half):
                pool.wait_ge(h_hi_done, at(2, m, half))
                low_part(h_lo[:], hid[:, half * HALF:(half + 1) * HALF, :], h_hi[:], h_lo_done)

            def output(b, odd):
                pool.wait_ge(zgelu_done, at(1, b, 0))
                G.tensor_tensor(rows_out[:], rows_out[:], x1[:, odd], ALU.add).then_inc(out_done, 1)

            def step(n, odd, e, edge=None):
                for k in range(TILES):
                    if k == 0 and running(edge, 0):
                        make_mask(n, 3, first=not had_one_before(edge, 0))
                    if k == 1 and not odd and running(edge, 2):
                        weight_lo(e, 1)
                    if k == 4 and running(edge, 3):
                        output(n - 3, 1 - odd)
                    if k == 4 and running(edge, 2):
                        h_low(n - 2, 0)
                    if k == 6 and running(edge, 1):
                        reciprocal_root(n - 1, LN2)
                    if k == 8 and running(edge, 1):
                        reciprocal_root(n - 1, LN3)
                    if k == 9 and running(edge, -1):
                        reciprocal_root(n + 1, LN1)
                        normalise_x(n + 1, 1 - odd, first=(edge == -1))
                    if k == 10 and running(edge, 1):
                        for c in range(DC):
                            pool.wait_ge(n_whole_done, at(DC, n - 1, c))
                            low_part(nT_lo[:, c, :], whole_T[:, c, :], nT_hi[:, c, :], nT_lo_done)
                    if k == 11 and running(edge, 2):
                        h_low(n - 2, 1)
                    if k == 12 and odd and running(edge, 1):
                        weight_lo(e, 0)
                    if k == 12 and running(edge, -1):
                        if edge == -1:
                            pool.wait_ge(small_in, 16 * 2)
                        add_b_o(n + 1, 1 - odd)
                    if k >= 13 and running(edge, -1):
                        make_mask(n + 1, k - 13, first=(edge == -1))

            G.memset(ident[:], 1.0).then_inc(consts_made, 1)
            G.memset(minus_half[:], -0.5).then_inc(pool_made, 1)
            pool.wait_ge(consts_made, 1)
            G.affine_select(out=ident[:], in_=ident[:], compare_op=ALU.is_equal, fill=0.0, base=0,
                            pattern=[[-1, P]], channel_multiplier=1).then_inc(consts_made, 1)
            pool.wait_ge(pool_made, 1)
            for n in range(-1, 3):
                step(n, n % 2, (n - 1) // 2 if n % 2 else n // 2 - 1, edge=n)
            with pool.Fori(0, EXPERTS - 2) as i:
                step(2 * i + 3, 1, i + 1)
                step(2 * i + 4, 0, i + 1)
            for n in range(LAST, LAST + 4):
                step(n, n % 2, (n - 1) // 2 if n % 2 else n // 2 - 1, edge=n)


def kernel(**inputs):
    import numpy as np
    import concourse.bacc as bacc
    from concourse.bass_utils import run_bass_kernel_spmd

    ins = {k: np.asarray(v) for k, v in inputs.items()}
    batches, tokens, d = ins["x"].shape
    experts = ins["L0_ffn_fc1_w"].shape[0]

    def by_expert(a):
        return np.ascontiguousarray(a.reshape(batches // experts, experts, *a.shape[1:]).swapaxes(0, 1)).reshape(a.shape)

    def as_columns(a):
        return a.reshape(-1, P).T

    vectors = ["L0_ffn_ln_g", "L0_ffn_ln_b", "L0_ffn_attn_b"]
    arrays = {
        "expert_columns": np.stack([np.concatenate([as_columns(b1), as_columns(b2)], axis=1)
                                    for b1, b2 in zip(ins["L0_ffn_fc1_b"], ins["L0_ffn_fc2_b"])]),
        "columns": np.concatenate([as_columns(ins[v]) for v in vectors], axis=1),
        "x": by_expert(ins["x"]),
        "adj": by_expert(ins["adj"]).view(np.uint32),
        "w_qkv": np.concatenate([ins["L0_gnn_Wq"], ins["L0_gnn_Wk"], ins["L0_gnn_Wv"]], axis=1),
        "w_o": ins["L0_gnn_Wo"],
        "b_o": ins["L0_gnn_bo"],
        "w_attn": ins["L0_ffn_attn_w"].T,
        "w_fc1": ins["L0_ffn_fc1_w"].transpose(0, 2, 1),
        "w_fc2": ins["L0_ffn_fc2_w"].transpose(0, 2, 1),
        "w_next": ins["L0_ffn_next_w"].T,
        "b_next": ins["L0_ffn_next_b"],
    }
    arrays = {k: np.ascontiguousarray(a) for k, a in arrays.items()}

    nc = bacc.Bacc("TRN2", target_bir_lowering=False, num_devices=1, dynamic_dma_scratch_size=1024)
    args = {k: nc.dram_tensor(f"in_{k}", a.shape, mybir.dt.from_np(a.dtype), kind="ExternalInput").ap()
            for k, a in arrays.items()}
    out = nc.dram_tensor("out", (batches, tokens, d), F32, kind="ExternalOutput").ap()
    build(nc, out=out, **args)
    r = run_bass_kernel_spmd(nc, [{f"in_{k}": a for k, a in arrays.items()}], core_ids=[0])
    got = r.results[0]["out"]
    return np.ascontiguousarray(got.reshape(experts, batches // experts, tokens, d).swapaxes(0, 1)).reshape(batches, tokens, d)
```

```python
from contextlib import ExitStack

import concourse.bass as bass
from concourse import mybir
from concourse.alu_op_type import AluOpType as ALU

F32 = mybir.dt.float32
F32R = mybir.dt.float32r
BF16 = mybir.dt.bfloat16
U8 = mybir.dt.uint8
U32 = mybir.dt.uint32
ACT = mybir.ActivationFunctionType

P = 128
EPS = 1e-5
MASKED = -(2.0**127)


def at(per_batch, batch, k):
    return batch * per_batch + (k + 1)


def build(nc, x, adj, columns, expert_columns, w_qkv, w_o, b_o, w_attn, w_fc1, w_fc2, w_next, b_next, out):
    BATCHES, TOKENS, D = x.shape
    EXPERTS, _, HID = w_fc1.shape
    HEADS = 4
    DH = D // HEADS
    QT = TOKENS // P
    DC = D // P
    HC = HID // P
    HALF = HC // 2
    PAIRS = HEADS // 2
    TILES = HEADS * QT
    SCALE = DH ** -0.5
    SLOTS = TILES + 4
    LAST = BATCHES - 1
    WORK_BANKS = 3
    HPARTS = HC // 2

    with ExitStack() as ctx:
        def sb(name, shape, dt=F32):
            return ctx.enter_context(nc.sbuf_tensor(name, shape, dt))

        def bank(name):
            return ctx.enter_context(nc.psum_tensor(name, [P, 512], F32))

        def sem(name):
            return ctx.enter_context(nc.semaphore(name))

        ident = sb("ident", [P, P])
        minus_half = sb("minus_half", [P, QT])
        cols = sb("cols", [P, columns.shape[1]])
        g_col = cols[:, 0:DC]
        b_col = cols[:, DC:2 * DC]
        battn_col = cols[:, 2 * DC:3 * DC]
        expert_cols = sb("expert_cols", [P, HC + DC])
        bfc1_col = expert_cols[:, 0:HC]
        bfc2_col = expert_cols[:, HC:HC + DC]
        bo_rows = sb("bo_rows", [P, D])
        bnext_rows = sb("bnext_rows", [P, D])
        wqkv_hi = sb("wqkv_hi", [P, DC, 3 * D], F32R)
        wqkv_lo = sb("wqkv_lo", [P, DC, 3 * D], F32R)
        wsq_hi = sb("wsq_hi", [P, 3, DC, D], F32R)
        wsq_lo = sb("wsq_lo", [P, 3, DC, D], F32R)
        W_O, W_ATTN, W_NEXT = 0, 1, 2
        fc1_hi = sb("fc1_hi", [P, DC, HID], F32R)
        fc1_lo = sb("fc1_lo", [P, DC, HID], F32R)
        fc2_hi = sb("fc2_hi", [P, HC, D], F32R)
        fc2_lo = sb("fc2_lo", [P, HC, D], F32R)
        w_raw = sb("w_raw", [P, DC * HID])

        x_in = sb("x_in", [P, 2, QT, D])
        adj_words = sb("adj_words", [P, QT, TOKENS // 4], U32)
        adj_u8 = adj_words[:].bitcast(U8)
        mask = sb("mask", [P, QT, TOKENS], BF16)
        normed = sb("normed", [P, QT, D])
        xT_hi = sb("xT_hi", [P, DC, TOKENS], F32R)
        xT_lo = sb("xT_lo", [P, DC, TOKENS], F32R)
        qk_hi = sb("qk_hi", [P, 2 * PAIRS, TOKENS], F32R)
        qk_lo = sb("qk_lo", [P, 2 * PAIRS, TOKENS], F32R)
        v_cat = sb("v_cat", [P, QT, HEADS, 2 * DH], F32R)
        probs = sb("probs", [P, 4, TOKENS])
        shift = sb("shift", [P, 4])
        total = sb("total", [P, 4])
        inv_total = sb("inv_total", [P, 4])
        pT_hi = sb("pT_hi", [P, QT, TOKENS], F32R)
        pT_lo = sb("pT_lo", [P, QT, TOKENS], F32R)
        o_f32 = sb("o_f32", [P, TOKENS])
        oT_hi = sb("oT_hi", [P, PAIRS, TOKENS], F32R)
        oT_lo = sb("oT_lo", [P, PAIRS, TOKENS], F32R)

        x1 = sb("x1", [P, 2, QT, D])
        y = sb("y", [P, QT, D])
        stats = sb("stats", [P, 3, QT, 6])
        moments = sb("moments", [P, 3, QT, 2])
        var_eps = sb("var_eps", [P, 3, QT])
        rstd = sb("rstd", [P, 3, QT])
        LN1, LN2, LN3 = 0, 1, 2
        nT_hi = sb("nT_hi", [P, DC, TOKENS], F32R)
        nT_lo = sb("nT_lo", [P, DC, TOKENS], F32R)
        whole_T = sb("whole_T", [P, DC, TOKENS])
        rows_out = sb("rows_out", [P, QT, D])
        y2_T = rows_out[:, :, :].rearrange("p t d -> p (t d)").rearrange("p (c q) -> p c q", c=DC)
        aT_hi = sb("aT_hi", [P, DC, TOKENS], F32R)
        aT_lo = sb("aT_lo", [P, DC, TOKENS], F32R)
        hid = sb("hid", [P, HC, TOKENS])
        yT = hid[:, 0:DC, :]
        h_hi = sb("h_hi", [P, HALF, TOKENS], F32R)
        h_lo = sb("h_lo", [P, HALF, TOKENS], F32R)

        score_ps = [bank(f"score_ps{i}") for i in range(2)]
        pT_ps = [bank(f"pT_ps{i}") for i in range(2)]
        o_ps = bank("o_ps")
        work_ps = [bank(f"work_ps{i}") for i in range(WORK_BANKS)]

        wqkv_in = sem("wqkv_in")
        wsq_in = sem("wsq_in")
        small_in = sem("small_in")
        consts_made = sem("consts_made")
        pool_made = sem("pool_made")
        wqkv_split = sem("wqkv_split")
        wsq_split = sem("wsq_split")
        x_in_dma = sem("x_in_dma")
        adj_in_dma = sem("adj_in_dma")
        wraw_dma = sem("wraw_dma")
        ecols_dma = sem("ecols_dma")
        w_hi_done = sem("w_hi_done")
        w_lo_done = sem("w_lo_done")
        rows_moved = sem("rows_moved")
        mask_done = sem("mask_done")
        stats_done = [sem(f"stats_done{i}") for i in range(3)]
        moments_done = [sem(f"moments_done{i}") for i in range(3)]
        eps_done = [sem(f"eps_done{i}") for i in range(3)]
        rstd_done = [sem(f"rstd_done{i}") for i in range(3)]
        xn_done = sem("xn_done")
        xbo_done = sem("xbo_done")
        y_done = sem("y_done")
        n_done = sem("n_done")
        xT_ready = sem("xT_ready")
        qk_ready = sem("qk_ready")
        v_ready = sem("v_ready")
        scores_ready = sem("scores_ready")
        pT_ready = sem("pT_ready")
        o_ready = sem("o_ready")
        wo_ready = sem("wo_ready")
        yT_ready = sem("yT_ready")
        nT_ready = sem("nT_ready")
        a_ready = sem("a_ready")
        fc1_ready = sem("fc1_ready")
        fc2_ready = sem("fc2_ready")
        next_ready = sem("next_ready")
        xT_hi_done = sem("xT_hi_done")
        qk_hi_done = sem("qk_hi_done")
        v_hi_done = sem("v_hi_done")
        exp_done = sem("exp_done")
        pT_hi_done = sem("pT_hi_done")
        o_second_taken = sem("o_second_taken")
        o_hi_done = sem("o_hi_done")
        yT_done = sem("yT_done")
        nT_hi_done = sem("nT_hi_done")
        a_hi_done = sem("a_hi_done")
        fc1_taken = sem("fc1_taken")
        gelu_done = sem("gelu_done")
        h_hi_done = sem("h_hi_done")
        fc2a_taken = sem("fc2a_taken")
        y2_hi_done = sem("y2_hi_done")
        zgelu_done = sem("zgelu_done")
        xT_lo_done = sem("xT_lo_done")
        qk_lo_done = sem("qk_lo_done")
        v_lo_done = sem("v_lo_done")
        masked_done = sem("masked_done")
        inv_done = sem("inv_done")
        probs_done = sem("probs_done")
        pT_lo_done = sem("pT_lo_done")
        o_added = sem("o_added")
        o_lo_done = sem("o_lo_done")
        x1_done = sem("x1_done")
        n_whole_done = sem("n_whole_done")
        a_whole_done = sem("a_whole_done")
        fc1_taken_dve = sem("fc1_taken_dve")
        a_lo_done = sem("a_lo_done")
        y2_done = sem("y2_done")
        y2_lo_done = sem("y2_lo_done")
        z_done = sem("z_done")
        out_done = sem("out_done")
        nT_lo_done = sem("nT_lo_done")
        h_lo_done = sem("h_lo_done")

        x_d = x.rearrange("b (t p) d -> b p t d", p=P)
        adj_d = adj.rearrange("b (t p) k -> b p t k", p=P)
        out_d = out.rearrange("b (t p) d -> b p t d", p=P)
        fc1_d = w_fc1.rearrange("e (c p) h -> e p c h", p=P)
        fc2_d = w_fc2.rearrange("e (c p) d -> e p c d", p=P)
        w_raw_fc1 = w_raw[:, :].rearrange("p (c h) -> p c h", c=DC)
        w_raw_fc2 = w_raw[:, :].rearrange("p (c d) -> p c d", c=HC)
        w_raw_qkv = w_raw[:, 0:DC * 3 * D].rearrange("p (c n) -> p c n", c=DC)
        w_raw_sq = hid[:, :, :].rearrange("p a b -> p (a b)")[:, 0:3 * DC * D].rearrange(
            "p (w c n) -> p w c n", w=3, c=DC)

        def f32(ap):
            return ap.bitcast(F32)

        dve_passed = sem("dve_passed")
        pool_passed = sem("pool_passed")
        sp_passed = sem("sp_passed")

        def wait_alone(engine, semaphore, value, passed):
            engine.wait_ge(semaphore, value)
            engine.sem_inc(passed, 1)

        block = ctx.enter_context(nc.Block())

        def running(edge, lag):
            return edge is None or 0 <= edge - lag <= LAST

        def had_one_before(edge, lag):
            return edge is None or edge - lag >= 1

        def tile_behind(k, d):
            return (0, k - d) if k >= d else (1, k - d + TILES)

        PRODUCTS = [
            [("fc1", 2, 2), ("qk", 2, 0)],
            [("fc1", 3, 2), ("qk", 3, 0)],
            [("fc1", 4, 2), ("fc1", 5, 2)],
            [("fc1", 6, 2)],
            [("fc1", 7, 2)],
            [("v", 0, 0), ("v", 1, 0)],
            [("wo", 0, 1), ("wo", 1, 1), ("fc2", 0, 2)],
            [("fc2", 1, 2)],
            [("yT", 0, 1), ("yT", 1, 1)],
            [("nT", 0, 1), ("nT", 1, 1)],
            [("fc2", 2, 2), ("fc2", 3, 2)],
            [("xT", 0, -1), ("xT", 1, -1)],
            [("attn", 0, 1), ("attn", 1, 1)],
            [("qk", 0, -1), ("fc1", 0, 1)],
            [("qk", 1, -1), ("fc1", 1, 1)],
            [("next", 0, 2), ("next", 1, 2)],
        ]
        TURNS = [(kind, j) for slot in PRODUCTS for kind, j, _ in slot]

        def bank_of(kind, j):
            return work_ps[TURNS.index((kind, j)) % WORK_BANKS]

        @block.sync
        def _(sp):
            def load_x(b, odd):
                wait_alone(sp, x1_done, at(2, b - 2, 1), sp_passed)
                sp.dma_start(x_in[:, odd], x_d[b]).then_inc(x_in_dma, 16)

            def load_adjacency(b):
                wait_alone(sp, mask_done, at(QT, b - 1, QT - 1), sp_passed)
                sp.dma_start(adj_words[:], adj_d[b]).then_inc(adj_in_dma, 16)

            def load_fc1(e, first):
                if first:
                    sp.wait_ge(wqkv_split, 2)
                else:
                    wait_alone(sp, w_lo_done, at(2, e - 1, 1), sp_passed)
                sp.dma_start(w_raw_fc1, fc1_d[e]).then_inc(wraw_dma, 16)

            def load_expert_columns(e, first):
                if not first:
                    wait_alone(sp, fc2a_taken, at(DC, 2 * e - 1, DC - 1), sp_passed)
                    wait_alone(sp, fc1_taken_dve, at(HALF, 2 * e - 1, HALF - 1), sp_passed)
                sp.dma_start(expert_cols[:], expert_columns[e]).then_inc(ecols_dma, 16)

            def load_fc2(e):
                wait_alone(sp, w_lo_done, at(2, e, 0), sp_passed)
                sp.dma_start(w_raw_fc2, fc2_d[e]).then_inc(wraw_dma, 16)

            def store(b):
                wait_alone(sp, out_done, at(1, b, 0), sp_passed)
                sp.dma_start(out_d[b], rows_out[:]).then_inc(rows_moved, 16)

            def step(n, odd, e, edge=None):
                if running(edge, -1):
                    load_adjacency(n + 1)
                if not odd and (edge is None or edge < 2 * (EXPERTS - 1) + 1):
                    load_fc1(e + 1, first=(edge == 0))
                if running(edge, 3):
                    store(n - 3)
                if running(edge, -1):
                    if edge == 0:
                        sp.wait_ge(stats_done[LN1], at(QT, 0, 0))
                        sp.dma_start(x_in[:, 1], x_d[1]).then_inc(x_in_dma, 16)
                    else:
                        load_x(n + 1, 1 - odd)
                if odd and (edge is None or edge <= LAST):
                    load_expert_columns(e, first=(edge == 1))
                    load_fc2(e)

            sp.dma_start(x_in[:, 0], x_d[0]).then_inc(x_in_dma, 16)
            sp.dma_start(w_raw_qkv, w_qkv.rearrange("(c p) n -> p c n", p=P)).then_inc(wqkv_in, 16)
            sp.dma_start(bo_rows[:], b_o.partition_broadcast(P)).then_inc(small_in, 16)
            sp.dma_start(adj_words[:], adj_d[0]).then_inc(adj_in_dma, 16)
            sp.dma_start(cols[:], columns).then_inc(small_in, 16)
            for w, src in ((W_O, w_o), (W_ATTN, w_attn), (W_NEXT, w_next)):
                sp.dma_start(w_raw_sq[:, w], src.rearrange("(c p) n -> p c n", p=P)).then_inc(wsq_in, 16)
            sp.dma_start(bnext_rows[:], b_next.partition_broadcast(P)).then_inc(rows_moved, 16)
            for n in range(0, 3):
                step(n, n % 2, (n - 1) // 2 if n % 2 else n // 2 - 1, edge=n)
            with sp.Fori(0, EXPERTS - 2) as i:
                step(2 * i + 3, 1, i + 1)
                step(2 * i + 4, 0, i + 1)
            for n in range(LAST, LAST + 4):
                step(n, n % 2, (n - 1) // 2 if n % 2 else n // 2 - 1, edge=n)
            sp.wait_ge(rows_moved, 16 * (BATCHES + 1))

        @block.tensor
        def _(pe):
            mm = nc.tensor.matmul

            def split_product(ps, lhs, rhs, blocks):
                passes = [(a, b, c) for c in range(blocks) for a, b in ((0, 0), (0, 1), (1, 0))]
                for i, (a, b, c) in enumerate(passes):
                    last = mm(ps, lhs[a](c), rhs[b](c), start=(i == 0), stop=(i == len(passes) - 1))
                return last

            def both(hi, lo, pick):
                return (lambda c: pick(hi, c)), (lambda c: pick(lo, c))

            def bank_read(kind, j, b):
                if kind == "fc1":
                    return (fc1_taken, at(HALF, b, j)) if j < HALF else (fc1_taken_dve, at(HALF, b, j - HALF))
                if kind == "fc2":
                    return (fc2a_taken, at(DC, b, j)) if j < DC else (y2_done, at(DC, b, j - DC))
                semaphore, count = {"xT": (xT_lo_done, DC), "qk": (qk_lo_done, 2 * PAIRS), "v": (v_lo_done, 2),
                                    "wo": (x1_done, 2), "yT": (yT_done, DC), "nT": (n_whole_done, DC),
                                    "attn": (a_whole_done, DC), "next": (z_done, 2)}[kind]
                return semaphore, at(count, b, j)

            def transposes(ps, src, c, ready):
                for t in range(QT):
                    last = nc.tensor.transpose(ps[:, t * P:(t + 1) * P], src[:, t, c * P:(c + 1) * P], ident[:])
                last.then_inc(ready, 1)

            def row_products(ps, u, lhs_hi, lhs_lo, rhs, ready):
                for i in range(2):
                    t = 2 * u + i
                    last = split_product(ps[:, i * D:(i + 1) * D],
                                         both(lhs_hi, lhs_lo, lambda a, c: a[:, c, t * P:(t + 1) * P]), rhs, DC)
                last.then_inc(ready, 1)

            def x_transposes(ps, b, c):
                if c == 0:
                    pe.wait_ge(xn_done, at(1, b, 0))
                transposes(ps, normed, c, xT_ready)

            def y_transposes(ps, b, c):
                if c == 0:
                    pe.wait_ge(y_done, at(1, b, 0))
                transposes(ps, y, c, yT_ready)

            def n_transposes(ps, b, c):
                if c == 0:
                    pe.wait_ge(n_done, at(1, b, 0))
                transposes(ps, y, c, nT_ready)

            def qk_products(ps, b, j):
                if j == 0:
                    pe.wait_ge(xT_lo_done, at(DC, b, DC - 1))
                col = (j % 2) * D + (j // 2) * P
                split_product(ps[:], both(wqkv_hi, wqkv_lo, lambda w, c: w[:, c, col:col + P]),
                              both(xT_hi, xT_lo, lambda w, c: w[:, c, :]), DC).then_inc(qk_ready, 1)

            def v_products(ps, b, u):
                row_products(ps, u, xT_hi, xT_lo, both(wqkv_hi, wqkv_lo, lambda w, c: w[:, c, 2 * D:3 * D]), v_ready)

            def wo_products(ps, b, u):
                if u == 0:
                    pe.wait_ge(o_lo_done, at(PAIRS, b, PAIRS - 1))
                row_products(ps, u, oT_hi, oT_lo, both(wsq_hi, wsq_lo, lambda w, c: w[:, W_O, c, :]), wo_ready)

            def next_products(ps, b, u):
                if u == 0:
                    pe.wait_ge(y2_lo_done, at(DC, b, DC - 1))
                row_products(ps, u, nT_hi, nT_lo, both(wsq_hi, wsq_lo, lambda w, c: w[:, W_NEXT, c, :]), next_ready)

            def attn_products(ps, b, c_out):
                if c_out == 0:
                    pe.wait_ge(nT_lo_done, at(DC, b, DC - 1))
                split_product(ps[:], both(wsq_hi, wsq_lo, lambda w, c: w[:, W_ATTN, c, c_out * P:(c_out + 1) * P]),
                              both(nT_hi, nT_lo, lambda w, c: w[:, c, :]), DC).then_inc(a_ready, 1)

            def fc1_products(ps, b, j):
                if j == 0:
                    pe.wait_ge(a_lo_done, at(DC, b, DC - 1))
                split_product(ps[:], both(fc1_hi, fc1_lo, lambda w, c: w[:, c, j * P:(j + 1) * P]),
                              both(aT_hi, aT_lo, lambda w, c: w[:, c, :]), DC).then_inc(fc1_ready, 1)

            def fc2_products(ps, b, j):
                def a_part_begins(i):
                    return i % (2 * 3) == 0

                half, c_out = divmod(j, DC)
                passes = [(w, h, c) for c in range(HALF)
                          for w, h in ((fc2_hi, h_hi), (fc2_hi, h_lo), (fc2_lo, h_hi))]
                for i, (w, h, c) in enumerate(passes):
                    if c_out == 0 and a_part_begins(i):
                        pe.wait_ge(h_lo_done, at(HPARTS, b, 2 * half + c // 2))
                    last = mm(ps[:], w[:, half * HALF + c, c_out * P:(c_out + 1) * P], h[:, c, :],
                              start=(i == 0), stop=(i == len(passes) - 1))
                last.then_inc(fc2_ready, 1)

            product = {"xT": x_transposes, "yT": y_transposes, "nT": n_transposes, "qk": qk_products,
                       "v": v_products, "wo": wo_products, "next": next_products, "attn": attn_products,
                       "fc1": fc1_products, "fc2": fc2_products}

            def scores(n, k, first):
                h, t = divmod(k, QT)
                pair, r = divmod(h, 2)
                if t == 0 and r == 0:
                    pe.wait_ge(qk_lo_done, at(2 * PAIRS, n, 2 * pair + 1))
                if k >= 2 or not first:
                    pe.wait_ge(masked_done, at(TILES, n, k - 2))
                rows = slice(DH * r, DH * (r + 1))
                ps = score_ps[k % 2]
                split_product(ps[:], both(qk_hi, qk_lo, lambda w, c: w[rows, 2 * pair, t * P:(t + 1) * P]),
                              both(qk_hi, qk_lo, lambda w, c: w[rows, 2 * pair + 1, :]), 1).then_inc(scores_ready, 1)

            def prob_transposes(b, k, first):
                pe.wait_ge(probs_done, at(TILES, b, k))
                if k >= 2 or not first:
                    pe.wait_ge(pT_lo_done, at(TILES, b, k - 2))
                ps = pT_ps[k % 2]
                for c in range(QT):
                    last = nc.tensor.transpose(ps[:, c * P:(c + 1) * P], probs[:, k % 4, c * P:(c + 1) * P], ident[:])
                last.then_inc(pT_ready, 1)

            def values(b, h, first):
                if h == 0:
                    pe.wait_ge(v_lo_done, at(2, b, 1))
                pe.wait_ge(pT_lo_done, at(TILES, b, QT * h + QT - 1))
                if h > 0 or not first:
                    pe.wait_ge(o_added, at(HEADS, b, h - 1))
                for c in range(QT):
                    mm(o_ps[:], v_cat[:, c, h, :], pT_hi[:, c, :], start=(c == 0), stop=False)
                    last = mm(o_ps[:], v_cat[:, c, h, :], pT_lo[:, c, :], start=False, stop=(c == QT - 1))
                last.then_inc(o_ready, 1)

            def step(n, odd, e, edge=None):
                if edge is None or edge == LAST:
                    for kind, j, lag in (PRODUCTS[-2] + PRODUCTS[-1])[-WORK_BANKS:]:
                        held[TURNS.index((kind, j)) % WORK_BANKS] = bank_read(kind, j, n - 1 - lag)
                for k in range(TILES):
                    if k % QT == 0:
                        lag, last_tile = tile_behind(k, 5)
                        if running(edge, lag):
                            values(n - lag, last_tile // QT, first=not had_one_before(edge, lag))
                    lag, tile = tile_behind(k, 3)
                    if running(edge, lag):
                        prob_transposes(n - lag, tile, first=not had_one_before(edge, lag))
                    for place, (kind, j, lag) in enumerate(PRODUCTS[k] + [(None, 0, 0)]):
                        if place == 1:
                            if k < TILES - 1 and running(edge, 0):
                                scores(n, k + 1, first=not had_one_before(edge, 0))
                            elif k == TILES - 1 and running(edge, -1):
                                scores(n + 1, 0, first=(edge == -1))
                        if kind is None or not running(edge, lag):
                            continue
                        if kind == "qk" and j == 0 and edge == -1:
                            pe.wait_ge(wqkv_split, 2)
                        if kind == "wo" and j == 0 and edge == 1:
                            pe.wait_ge(wsq_split, 2)
                        if kind == "fc1" and j == 0 and odd:
                            pe.wait_ge(w_lo_done, at(2, e, 0))
                        if kind == "fc2" and j == 0 and not odd:
                            pe.wait_ge(w_lo_done, at(2, e, 1))
                        i = TURNS.index((kind, j)) % WORK_BANKS
                        if held[i] is not None:
                            pe.wait_ge(*held[i])
                        held[i] = bank_read(kind, j, n - lag)
                        product[kind](bank_of(kind, j), n - lag, j)

            held = [None] * WORK_BANKS
            pe.wait_ge(consts_made, 2)
            for n in range(-1, 3):
                step(n, n % 2, (n - 1) // 2 if n % 2 else n // 2 - 1, edge=n)
            with pe.Fori(0, EXPERTS - 2) as i:
                step(2 * i + 3, 1, i + 1)
                step(2 * i + 4, 0, i + 1)
            for n in range(LAST, LAST + 4):
                step(n, n % 2, (n - 1) // 2 if n % 2 else n // 2 - 1, edge=n)

        @block.scalar
        def _(act):
            A = nc.scalar.activation

            def x_hi(b, c):
                act.wait_ge(xT_ready, at(DC, b, c))
                A(xT_hi[:, c, :], bank_of("xT", c)[:], ACT.Copy).then_inc(xT_hi_done, 1)

            def qk_high(b, j):
                act.wait_ge(qk_ready, at(2 * PAIRS, b, j))
                A(qk_hi[:, j, :], bank_of("qk", j)[:], ACT.Copy).then_inc(qk_hi_done, 1)

            def v_high(b, u):
                act.wait_ge(v_ready, at(2, b, u))
                A(v_cat[:, 2 * u:2 * u + 2, :, 0:DH],
                  bank_of("v", u)[:].rearrange("p (t h d) -> p t h d", t=2, h=HEADS), ACT.Copy).then_inc(v_hi_done, 1)

            def exponentials(n, k):
                act.wait_ge(masked_done, at(TILES, n, k))
                A(probs[:, k % 4, :], probs[:, k % 4, :], ACT.Exp, bias=shift[:, k % 4:k % 4 + 1], scale=-1.0,
                  accum_out=total[:, k % 4:k % 4 + 1]).then_inc(exp_done, 1)

            def prob_hi(b, k, first):
                h, t = divmod(k, QT)
                act.wait_ge(pT_ready, at(TILES, b, k))
                if t == 0 and (h > 0 or not first):
                    act.wait_ge(o_ready, at(HEADS, b, h - 1))
                A(pT_hi[:, :, t * P:(t + 1) * P], pT_ps[k % 2][:].rearrange("p (c q) -> p c q", c=QT),
                  ACT.Copy).then_inc(pT_hi_done, 1)

            def take_second_half(b, h, first):
                pair, r = divmod(h, 2)
                act.wait_ge(o_ready, at(HEADS, b, h))
                if r == 0 and (pair > 0 or not first):
                    act.wait_ge(o_lo_done, at(PAIRS, b, pair - 1))
                A(o_f32[DH * r:DH * (r + 1), :], o_ps[DH:2 * DH, :], ACT.Copy).then_inc(o_second_taken, 1)

            def o_hi(b, pair):
                act.wait_ge(o_added, at(HEADS, b, 2 * pair + 1))
                A(oT_hi[:, pair, :], o_f32[:], ACT.Copy).then_inc(o_hi_done, 1)

            def n_hi(m, c):
                act.wait_ge(nT_ready, at(DC, m, c))
                A(nT_hi[:, c, :], bank_of("nT", c)[:], ACT.Identity, bias=b_col[:, c:c + 1],
                  scale=g_col[:, c:c + 1]).then_inc(nT_hi_done, 1)

            def a_hi(m, c):
                act.wait_ge(a_whole_done, at(DC, m, c))
                A(aT_hi[:, c, :], whole_T[:, c, :], ACT.Copy).then_inc(a_hi_done, 1)

            def fc1_take(m, j):
                act.wait_ge(fc1_ready, at(HC, m, j))
                A(hid[:, j, :], bank_of("fc1", j)[:], ACT.Identity,
                  bias=bfc1_col[:, j:j + 1]).then_inc(fc1_taken, 1)

            def gelu(m, half):
                done = fc1_taken_dve if half else fc1_taken
                act.wait_ge(done, at(HALF, m, HALF - 1))
                rows = slice(half * HALF, (half + 1) * HALF)
                A(hid[:, rows, :], hid[:, rows, :], ACT.Gelu).then_inc(gelu_done, 1)

            def h_high(m, part):
                half, i = divmod(part, 2)
                if i == 0:
                    act.wait_ge(gelu_done, at(2, m, half))
                if part == 2:
                    act.wait_ge(fc2_ready, at(2 * DC, m, DC - 1))
                A(h_hi[:, 2 * i:2 * i + 2, :], hid[:, 2 * part:2 * part + 2, :], ACT.Copy).then_inc(h_hi_done, 1)

            def fc2a_take(m, c):
                if c == 0:
                    act.wait_ge(rows_moved, 16 * at(1, m, 0))
                act.wait_ge(fc2_ready, at(2 * DC, m, c))
                A(y2_T[:, c, :], bank_of("fc2", c)[:], ACT.Identity,
                  bias=bfc2_col[:, c:c + 1]).then_inc(fc2a_taken, 1)

            def y2_hi(m, c):
                act.wait_ge(y2_done, at(DC, m, c))
                A(nT_hi[:, c, :], y2_T[:, c, :], ACT.Copy).then_inc(y2_hi_done, 1)

            def z_gelu(b):
                act.wait_ge(z_done, at(2, b, 1))
                A(rows_out[:], rows_out[:], ACT.Gelu).then_inc(zgelu_done, 1)

            def weight_hi(e, which, first):
                act.wait_ge(wraw_dma, 16 * (2 * e + which + 1))
                if not first:
                    b = 2 * e - 1
                    if which == 0:
                        act.wait_ge(fc1_ready, at(HC, b, HC - 1))
                    else:
                        act.wait_ge(fc2_ready, at(2 * DC, b, 2 * DC - 1))
                dst, src = (fc1_hi, w_raw_fc1) if which == 0 else (fc2_hi, w_raw_fc2)
                A(dst[:], src, ACT.Copy).then_inc(w_hi_done, 1)

            H_HIGH_SLOTS = (4, 5, 8, 8)

            def step(n, odd, e, edge=None):
                for k in range(TILES):
                    lag, tile = tile_behind(k, 4)
                    if running(edge, lag):
                        prob_hi(n - lag, tile, first=not had_one_before(edge, lag))
                    if k == 3:
                        if running(edge, 3):
                            z_gelu(n - 3)
                        if running(edge, 2):
                            gelu(n - 2, 0)
                    if running(edge, 0):
                        exponentials(n, k)
                    if k % QT == 0:
                        lag, last_tile = tile_behind(k, 5)
                        if running(edge, lag):
                            take_second_half(n - lag, last_tile // QT, first=not had_one_before(edge, lag))

                    if k == 0:
                        if running(edge, 2):
                            fc1_take(n - 2, 2)
                        if running(edge, 0):
                            qk_high(n, 2)
                        if not odd and running(edge, 2):
                            weight_hi(e, 1, first=(edge == 2))
                    elif k == 1:
                        if running(edge, 2):
                            fc1_take(n - 2, 3)
                        if running(edge, 0):
                            qk_high(n, 3)
                    elif k == 5:
                        if running(edge, 1):
                            o_hi(n - 1, 1)
                        if running(edge, 0):
                            v_high(n, 0)
                            v_high(n, 1)
                    elif k == 6 and running(edge, 2):
                        gelu(n - 2, 1)
                        fc2a_take(n - 2, 0)
                    elif k == 7:
                        if running(edge, 2):
                            fc2a_take(n - 2, 1)
                        if odd and running(edge, 1):
                            weight_hi(e, 0, first=(edge == 1))
                    elif k == 9 and running(edge, 1):
                        n_hi(n - 1, 0)
                        n_hi(n - 1, 1)
                    elif k == 11 and running(edge, -1):
                        x_hi(n + 1, 0)
                        x_hi(n + 1, 1)
                    elif k == 12 and running(edge, 1):
                        a_hi(n - 1, 0)
                        a_hi(n - 1, 1)
                    elif k == 13:
                        if running(edge, -1):
                            qk_high(n + 1, 0)
                        if running(edge, 1):
                            if odd:
                                act.wait_ge(ecols_dma, 16 * (e + 1))
                            fc1_take(n - 1, 0)
                        if running(edge, 0):
                            o_hi(n, 0)
                        if running(edge, 2):
                            y2_hi(n - 2, 0)
                            y2_hi(n - 2, 1)
                    elif k == 14:
                        if running(edge, -1):
                            qk_high(n + 1, 1)
                        if running(edge, 1):
                            fc1_take(n - 1, 1)
                    for part, slot in enumerate(H_HIGH_SLOTS):
                        if k == slot and running(edge, 2):
                            h_high(n - 2, part)

            act.wait_ge(wqkv_in, 16)
            A(wqkv_hi[:], w_raw_qkv, ACT.Copy).then_inc(wqkv_split, 1)
            step(-1, 1, None, edge=-1)
            act.wait_ge(wsq_in, 16 * 3)
            A(wsq_hi[:], w_raw_sq, ACT.Copy).then_inc(wsq_split, 1)
            act.wait_ge(small_in, 16 * 2)
            for n in range(0, 3):
                step(n, n % 2, (n - 1) // 2 if n % 2 else n // 2 - 1, edge=n)
            with act.Fori(0, EXPERTS - 2) as i:
                step(2 * i + 3, 1, i + 1)
                step(2 * i + 4, 0, i + 1)
            for n in range(LAST, LAST + 4):
                step(n, n % 2, (n - 1) // 2 if n % 2 else n // 2 - 1, edge=n)

        @block.vector
        def _(dve):
            V = nc.vector

            def row_stats(b, which, src):
                for t in range(QT):
                    V.bn_stats(stats[:, which, t, :], src[:, t, :]).then_inc(stats_done[which], 1)
                wait_alone(dve, stats_done[which], at(QT, b, QT - 1), dve_passed)
                for t in range(QT):
                    last = V.bn_aggr(moments[:, which, t, :], stats[:, which, t, :])
                last.then_inc(moments_done[which], 1)

            def normalise(b, which, src, dst, done):
                dve.wait_ge(rstd_done[which], at(1, b, 0))
                for t in range(QT):
                    last = V.tensor_scalar(dst[:, t, :], src[:, t, :], moments[:, which, t, 0:1],
                                           rstd[:, which, t:t + 1], ALU.subtract, ALU.mult)
                last.then_inc(done, 1)

            def low_part(dst, src, hi, done):
                V.tensor_tensor(dst, src, f32(hi), ALU.subtract).then_inc(done, 1)

            def x_lo(b, c):
                dve.wait_ge(xT_hi_done, at(DC, b, c))
                low_part(xT_lo[:, c, :], bank_of("xT", c)[:], xT_hi[:, c, :], xT_lo_done)

            def qk_low(b, j):
                dve.wait_ge(qk_hi_done, at(2 * PAIRS, b, j))
                low_part(qk_lo[:, j, :], bank_of("qk", j)[:], qk_hi[:, j, :], qk_lo_done)

            def v_low(b, u):
                dve.wait_ge(v_hi_done, at(2, b, u))
                tt = slice(2 * u, 2 * u + 2)
                low_part(v_cat[:, tt, :, DH:2 * DH],
                         bank_of("v", u)[:].rearrange("p (t h d) -> p t h d", t=2, h=HEADS),
                         v_cat[:, tt, :, 0:DH], v_lo_done)

            def mask_and_max(n, k, first):
                t = k % QT
                if k < QT:
                    wait_alone(dve, mask_done, at(QT, n, t), dve_passed)
                if k >= 4 or not first:
                    wait_alone(dve, pT_ready, at(TILES, n, k - 4), dve_passed)
                wait_alone(dve, scores_ready, at(TILES, n, k), dve_passed)
                V.tensor_tensor_reduce(out=probs[:, k % 4, :], in0=score_ps[k % 2][:], in1=mask[:, t, :],
                                       scale=-SCALE, scalar=3.0e38, op0=ALU.add, op1=ALU.min,
                                       accum_out=shift[:, k % 4:k % 4 + 1]).then_inc(masked_done, 1)

            def invert_total(b, k):
                dve.wait_ge(exp_done, at(TILES, b, k))
                V.reciprocal(inv_total[:, k % 4:k % 4 + 1], total[:, k % 4:k % 4 + 1]).then_inc(inv_done, 1)

            def normalise_probs(b, k):
                dve.wait_ge(inv_done, at(TILES, b, k))
                V.tensor_scalar(probs[:, k % 4, :], probs[:, k % 4, :], inv_total[:, k % 4:k % 4 + 1], None,
                                ALU.mult).then_inc(probs_done, 1)

            def prob_lo(b, k):
                t = k % QT
                dve.wait_ge(pT_hi_done, at(TILES, b, k))
                low_part(pT_lo[:, :, t * P:(t + 1) * P], pT_ps[k % 2][:].rearrange("p (c q) -> p c q", c=QT),
                         pT_hi[:, :, t * P:(t + 1) * P], pT_lo_done)

            def add_halves(b, h):
                rows = slice(DH * (h % 2), DH * (h % 2 + 1))
                dve.wait_ge(o_second_taken, at(HEADS, b, h))
                V.tensor_tensor(o_f32[rows, :], o_ps[0:DH, :], o_f32[rows, :], ALU.add).then_inc(o_added, 1)

            def o_lo(b, pair):
                dve.wait_ge(o_hi_done, at(PAIRS, b, pair))
                low_part(oT_lo[:, pair, :], o_f32[:], oT_hi[:, pair, :], o_lo_done)

            def residual(b, odd, u, half_was_used):
                if u == 0:
                    dve.wait_ge(xbo_done, at(1, b, 0))
                    if half_was_used:
                        dve.wait_ge(out_done, at(1, b - 2, 0))
                dve.wait_ge(wo_ready, at(2, b, u))
                tt = slice(2 * u, 2 * u + 2)
                V.tensor_tensor(x1[:, odd, tt, :], bank_of("wo", u)[:].rearrange("p (t d) -> p t d", t=2),
                                x_in[:, odd, tt, :], ALU.add).then_inc(x1_done, 1)

            def y_take(m, c):
                dve.wait_ge(yT_ready, at(DC, m, c))
                V.tensor_scalar(yT[:, c, :], bank_of("yT", c)[:], battn_col[:, c:c + 1], None,
                                ALU.add).then_inc(yT_done, 1)

            def n_whole(m, c):
                dve.wait_ge(nT_hi_done, at(DC, m, c))
                V.tensor_scalar(whole_T[:, c, :], bank_of("nT", c)[:], g_col[:, c:c + 1], b_col[:, c:c + 1],
                                ALU.mult, ALU.add).then_inc(n_whole_done, 1)

            def a_whole(m, c):
                dve.wait_ge(a_ready, at(DC, m, c))
                dve.wait_ge(yT_done, at(DC, m, c))
                dve.wait_ge(nT_lo_done, at(DC, m, c))
                V.tensor_tensor(whole_T[:, c, :], bank_of("attn", c)[:], yT[:, c, :],
                                ALU.add).then_inc(a_whole_done, 1)

            def a_lo(m, c):
                dve.wait_ge(a_hi_done, at(DC, m, c))
                low_part(aT_lo[:, c, :], whole_T[:, c, :], aT_hi[:, c, :], a_lo_done)

            def fc1_take(m, j):
                dve.wait_ge(fc1_ready, at(HC, m, j))
                V.tensor_scalar(hid[:, j, :], bank_of("fc1", j)[:], bfc1_col[:, j:j + 1], None,
                                ALU.add).then_inc(fc1_taken_dve, 1)

            def y2_whole(m, c):
                dve.wait_ge(fc2_ready, at(2 * DC, m, DC + c))
                dve.wait_ge(fc2a_taken, at(DC, m, c))
                V.tensor_tensor(y2_T[:, c, :], bank_of("fc2", DC + c)[:], y2_T[:, c, :],
                                ALU.add).then_inc(y2_done, 1)

            def y2_lo(m, c):
                dve.wait_ge(y2_hi_done, at(DC, m, c))
                low_part(nT_lo[:, c, :], y2_T[:, c, :], nT_hi[:, c, :], y2_lo_done)

            def h_low(m, half):
                for i in range(2):
                    part = 2 * half + i
                    dve.wait_ge(h_hi_done, at(HPARTS, m, part))
                    low_part(h_lo[:, 2 * i:2 * i + 2, :], hid[:, 2 * part:2 * part + 2, :],
                             h_hi[:, 2 * i:2 * i + 2, :], h_lo_done)

            def z_take(b, u):
                dve.wait_ge(next_ready, at(2, b, u))
                V.tensor_tensor(rows_out[:, 2 * u:2 * u + 2, :],
                                bank_of("next", u)[:].rearrange("p (t d) -> p t d", t=2),
                                bnext_rows[:, :].unsqueeze(1).broadcast_to([P, 2, D]),
                                ALU.add).then_inc(z_done, 1)

            def step(n, odd, e, edge=None):
                for k in range(TILES):
                    lag, tile = tile_behind(k, 1)
                    if running(edge, lag):
                        invert_total(n - lag, tile)
                    lag, tile = tile_behind(k, 4)
                    if running(edge, lag):
                        prob_lo(n - lag, tile)
                    lag, tile = tile_behind(k, 1)
                    if running(edge, lag):
                        normalise_probs(n - lag, tile)
                    if k % QT == 0:
                        lag, last_tile = tile_behind(k, 5)
                        if running(edge, lag):
                            add_halves(n - lag, last_tile // QT)
                    if k == 8 and running(edge, 1):
                        dve.wait_ge(yT_ready, at(DC, n - 1, DC - 1))
                        normalise(n - 1, LN3, y, y, n_done)
                    if k < TILES - 1 and running(edge, 0):
                        mask_and_max(n, k + 1, first=not had_one_before(edge, 0))
                    elif k == TILES - 1 and running(edge, -1):
                        mask_and_max(n + 1, 0, first=(edge == -1))

                    if k in (5, 8) and edge is not None and edge > LAST and running(edge, 2):
                        h_low(n - 2, k // 8)
                    if k in (0, 1) and running(edge, 0):
                        qk_low(n, 2 + k)
                    elif k in (2, 3, 4) and running(edge, 2):
                        if k == 2:
                            if not odd:
                                dve.wait_ge(ecols_dma, 16 * (e + 1))
                            fc1_take(n - 2, 4)
                        fc1_take(n - 2, k + 3)
                    elif k == 5:
                        if running(edge, 1):
                            o_lo(n - 1, 1)
                        if running(edge, 0):
                            v_low(n, 0)
                            v_low(n, 1)
                    elif k == 6 and running(edge, 1):
                        residual(n - 1, 1 - odd, 0, running(edge, 3))
                        residual(n - 1, 1 - odd, 1, running(edge, 3))
                        wait_alone(dve, x1_done, at(2, n - 1, 1), dve_passed)
                        row_stats(n - 1, LN2, x1[:, 1 - odd])
                    elif k == 7 and running(edge, 1):
                        normalise(n - 1, LN2, x1[:, 1 - odd], y, y_done)
                        wait_alone(dve, y_done, at(1, n - 1, 0), dve_passed)
                        row_stats(n - 1, LN3, y)
                    elif k == 8 and running(edge, 1):
                        y_take(n - 1, 0)
                        y_take(n - 1, 1)
                    elif k == 9:
                        if running(edge, -1):
                            wait_alone(dve, x_in_dma, 16 * (n + 2), dve_passed)
                            row_stats(n + 1, LN1, x_in[:, 1 - odd])
                        if running(edge, 1):
                            n_whole(n - 1, 0)
                            n_whole(n - 1, 1)
                    elif k == 10:
                        if running(edge, -1):
                            if edge != -1:
                                dve.wait_ge(xT_ready, at(DC, n, DC - 1))
                            normalise(n + 1, LN1, x_in[:, 1 - odd], normed, xn_done)
                        if running(edge, 2):
                            y2_whole(n - 2, 0)
                    elif k == 11:
                        if edge == -1:
                            dve.wait_ge(wqkv_in, 16)
                            dve.wait_ge(wqkv_split, 1)
                            V.tensor_tensor(wqkv_lo[:], w_raw_qkv, f32(wqkv_hi[:]),
                                            ALU.subtract).then_inc(wqkv_split, 1)
                        if running(edge, 2):
                            y2_whole(n - 2, 1)
                        if running(edge, -1):
                            x_lo(n + 1, 0)
                            x_lo(n + 1, 1)
                    elif k == 12 and running(edge, 1):
                        a_whole(n - 1, 0)
                        a_whole(n - 1, 1)
                        a_lo(n - 1, 0)
                        a_lo(n - 1, 1)
                    elif k == 13:
                        if running(edge, -1):
                            qk_low(n + 1, 0)
                        if running(edge, 0):
                            o_lo(n, 0)
                        if running(edge, 2):
                            y2_lo(n - 2, 0)
                            y2_lo(n - 2, 1)
                    elif k == 14 and running(edge, -1):
                        qk_low(n + 1, 1)
                    elif k == 15 and running(edge, 2):
                        z_take(n - 2, 0)
                        z_take(n - 2, 1)

            dve.wait_ge(x_in_dma, 16)
            step(-1, 1, None, edge=-1)
            dve.wait_ge(wsq_in, 16 * 3)
            dve.wait_ge(wsq_split, 1)
            V.tensor_tensor(wsq_lo[:], w_raw_sq, f32(wsq_hi[:]), ALU.subtract).then_inc(wsq_split, 1)
            dve.wait_ge(small_in, 16 * 2)
            for n in range(0, 3):
                step(n, n % 2, (n - 1) // 2 if n % 2 else n // 2 - 1, edge=n)
            with dve.Fori(0, EXPERTS - 2) as i:
                step(2 * i + 3, 1, i + 1)
                step(2 * i + 4, 0, i + 1)
            for n in range(LAST, LAST + 4):
                step(n, n % 2, (n - 1) // 2 if n % 2 else n // 2 - 1, edge=n)

        @block.gpsimd
        def _(pool):
            G = nc.gpsimd

            def reciprocal_root(b, which):
                wait_alone(pool, moments_done[which], at(1, b, 0), pool_passed)
                G.tensor_scalar(var_eps[:, which, :], moments[:, which, :, 1], EPS, None,
                                ALU.add).then_inc(eps_done[which], 1)
                pool.wait_ge(eps_done[which], at(1, b, 0))
                G.tensor_tensor(rstd[:, which, :], var_eps[:, which, :], minus_half[:],
                                ALU.pow).then_inc(rstd_done[which], 1)

            def add_b_o(b, odd):
                pool.wait_ge(xn_done, at(1, b, 0))
                G.tensor_tensor(x_in[:, odd], x_in[:, odd], bo_rows[:, :].unsqueeze(1).broadcast_to([P, QT, D]),
                                ALU.add).then_inc(xbo_done, 1)

            def make_mask(b, t, first):
                if t == 0:
                    wait_alone(pool, adj_in_dma, 16 * (b + 1), pool_passed)
                if not first:
                    wait_alone(pool, masked_done, at(TILES, b, t - QT), pool_passed)
                G.tensor_scalar(mask[:, t, :], adj_u8[:, t, :], -1.0, -MASKED, ALU.add,
                                ALU.mult).then_inc(mask_done, 1)

            def low_part(dst, src, hi, done):
                G.tensor_tensor(dst, src, f32(hi), ALU.subtract).then_inc(done, 1)

            def weight_lo(e, which):
                pool.wait_ge(w_hi_done, at(2, e, which))
                dst, src, hi = (fc1_lo, w_raw_fc1, fc1_hi) if which == 0 else (fc2_lo, w_raw_fc2, fc2_hi)
                low_part(dst[:], src, hi[:], w_lo_done)

            def h_low(m, half):
                for i in range(2):
                    part = 2 * half + i
                    pool.wait_ge(h_hi_done, at(HPARTS, m, part))
                    low_part(h_lo[:, 2 * i:2 * i + 2, :], hid[:, 2 * part:2 * part + 2, :],
                             h_hi[:, 2 * i:2 * i + 2, :], h_lo_done)

            def output(b, odd):
                pool.wait_ge(zgelu_done, at(1, b, 0))
                G.tensor_tensor(rows_out[:], rows_out[:], x1[:, odd], ALU.add).then_inc(out_done, 1)

            def step(n, odd, e, edge=None):
                for k in range(TILES):
                    if k == 0 and running(edge, 0):
                        make_mask(n, 3, first=not had_one_before(edge, 0))
                    if k == 1 and not odd and running(edge, 2):
                        weight_lo(e, 1)
                    if k == 2 and running(edge, 3):
                        output(n - 3, 1 - odd)
                    if k == 3 and running(edge, 2) and (edge is None or edge <= LAST):
                        h_low(n - 2, 0)
                    if k == 6 and running(edge, 1):
                        reciprocal_root(n - 1, LN2)
                    if k == 7 and running(edge, 1):
                        reciprocal_root(n - 1, LN3)
                    if k == 8 and running(edge, 2) and (edge is None or edge <= LAST):
                        h_low(n - 2, 1)
                    if k == 9 and running(edge, -1):
                        reciprocal_root(n + 1, LN1)
                    if k == 9 and running(edge, 1):
                        for c in range(DC):
                            pool.wait_ge(n_whole_done, at(DC, n - 1, c))
                            low_part(nT_lo[:, c, :], whole_T[:, c, :], nT_hi[:, c, :], nT_lo_done)
                    if k == 10 and odd and running(edge, 1):
                        weight_lo(e, 0)
                    if k == 12 and running(edge, -1):
                        if edge == -1:
                            pool.wait_ge(small_in, 16 * 2)
                        add_b_o(n + 1, 1 - odd)
                    if k >= 13 and running(edge, -1):
                        make_mask(n + 1, k - 13, first=(edge == -1))

            G.memset(ident[:], 1.0).then_inc(consts_made, 1)
            G.memset(minus_half[:], -0.5).then_inc(pool_made, 1)
            pool.wait_ge(consts_made, 1)
            G.affine_select(out=ident[:], in_=ident[:], compare_op=ALU.is_equal, fill=0.0, base=0,
                            pattern=[[-1, P]], channel_multiplier=1).then_inc(consts_made, 1)
            pool.wait_ge(pool_made, 1)
            for n in range(-1, 3):
                step(n, n % 2, (n - 1) // 2 if n % 2 else n // 2 - 1, edge=n)
            with pool.Fori(0, EXPERTS - 2) as i:
                step(2 * i + 3, 1, i + 1)
                step(2 * i + 4, 0, i + 1)
            for n in range(LAST, LAST + 4):
                step(n, n % 2, (n - 1) // 2 if n % 2 else n // 2 - 1, edge=n)


def kernel(**inputs):
    import numpy as np
    import concourse.bacc as bacc
    from concourse.bass_utils import run_bass_kernel_spmd

    ins = {k: np.asarray(v) for k, v in inputs.items()}
    batches, tokens, d = ins["x"].shape
    experts = ins["L0_ffn_fc1_w"].shape[0]

    def by_expert(a):
        return np.ascontiguousarray(a.reshape(batches // experts, experts, *a.shape[1:]).swapaxes(0, 1)).reshape(a.shape)

    def as_columns(a):
        return a.reshape(-1, P).T

    vectors = ["L0_ffn_ln_g", "L0_ffn_ln_b", "L0_ffn_attn_b"]
    arrays = {
        "expert_columns": np.stack([np.concatenate([as_columns(b1), as_columns(b2)], axis=1)
                                    for b1, b2 in zip(ins["L0_ffn_fc1_b"], ins["L0_ffn_fc2_b"])]),
        "columns": np.concatenate([as_columns(ins[v]) for v in vectors], axis=1),
        "x": by_expert(ins["x"]),
        "adj": by_expert(ins["adj"]).view(np.uint32),
        "w_qkv": np.concatenate([ins["L0_gnn_Wq"], ins["L0_gnn_Wk"], ins["L0_gnn_Wv"]], axis=1),
        "w_o": ins["L0_gnn_Wo"],
        "b_o": ins["L0_gnn_bo"],
        "w_attn": ins["L0_ffn_attn_w"].T,
        "w_fc1": ins["L0_ffn_fc1_w"].transpose(0, 2, 1),
        "w_fc2": ins["L0_ffn_fc2_w"].transpose(0, 2, 1),
        "w_next": ins["L0_ffn_next_w"].T,
        "b_next": ins["L0_ffn_next_b"],
    }
    arrays = {k: np.ascontiguousarray(a) for k, a in arrays.items()}

    nc = bacc.Bacc("TRN2", target_bir_lowering=False, num_devices=1, dynamic_dma_scratch_size=1024)
    args = {k: nc.dram_tensor(f"in_{k}", a.shape, mybir.dt.from_np(a.dtype), kind="ExternalInput").ap()
            for k, a in arrays.items()}
    out = nc.dram_tensor("out", (batches, tokens, d), F32, kind="ExternalOutput").ap()
    build(nc, out=out, **args)
    r = run_bass_kernel_spmd(nc, [{f"in_{k}": a for k, a in arrays.items()}], core_ids=[0])
    got = r.results[0]["out"]
    return np.ascontiguousarray(got.reshape(experts, batches // experts, tokens, d).swapaxes(0, 1)).reshape(batches, tokens, d)
```
